# Optimizing a Trainium2 kernel written in Bass

```python
import numpy as np
import jax
import jax.numpy as jnp

def _softmax(x, axis=-1):
    return jax.nn.softmax(x, axis=axis)

def _gelu(x):
    return jax.nn.gelu(x, approximate=True)

def _silu(x):
    return jax.nn.silu(x)

def _sigmoid(x):
    return jax.nn.sigmoid(x)

def _layernorm(x, axis=-1, eps=1e-05):
    m = jnp.mean(x, axis=axis, keepdims=True)
    v = jnp.var(x, axis=axis, keepdims=True)
    return (x - m) / jnp.sqrt(v + eps)

def _scatter_add(tgt, idx, src, axis=0):
    return tgt.at[idx].add(src)

def _segment_sum(src, seg, n):
    return jax.ops.segment_sum(src, seg, n)
kernel_name = 'mk_prb_d1_jaxref_r8_15db8b'

def setup_inputs(seed: int=0):
    np.random.seed(seed)
    _w = jnp.asarray

    def _L0_attn_setup():
        import jax, jax.numpy as jnp
        import numpy as np
        B, S, D, H = (4, 256, 128, 16)
        DK = D // H

        def apply_rope(x, pos, inv_freq):
            sincos = pos[:, :, None].astype(jnp.float32) * inv_freq
            sin = jnp.repeat(jnp.sin(sincos), 2, axis=-1)[:, None]
            cos = jnp.repeat(jnp.cos(sincos), 2, axis=-1)[:, None]
            x_rot = jnp.stack([-x[..., 1::2], x[..., ::2]], axis=-1).reshape(x.shape)
            return x * cos + x_rot * sin
        key = jax.random.key(seed)
        ks = jax.random.split(key, 5)
        scale = 1.0 / np.sqrt(D)
        x = jax.random.normal(ks[0], (B, S, D), dtype=jnp.float32)
        W_q = jax.random.normal(ks[1], (D, D), dtype=jnp.float32) * scale
        W_k = jax.random.normal(ks[2], (D, D), dtype=jnp.float32) * scale
        W_v = jax.random.normal(ks[3], (D, D), dtype=jnp.float32) * scale
        W_o = jax.random.normal(ks[4], (D, D), dtype=jnp.float32) * scale
        return {'x': x, 'W_q': W_q, 'W_k': W_k, 'W_v': W_v, 'W_o': W_o}
    _L0_attn_in = _L0_attn_setup()

    def _L0_ffn_setup():
        import jax, jax.numpy as jnp
        import numpy as np
        E, K, D, F = (8, 2, 128, 512)
        EPS = 1e-06
        B, S = (2, 128)
        key = jax.random.key(seed)
        ks = jax.random.split(key, 6)
        s_in = 1.0 / np.sqrt(D)
        s_mid = 1.0 / np.sqrt(F)
        return {'x': jax.random.normal(ks[0], (B, S, D), dtype=jnp.float32), 'Wg': jax.random.normal(ks[1], (D, E), dtype=jnp.float32) * s_in, 'gamma': jnp.ones((E, D), dtype=jnp.float32), 'beta': jnp.zeros((E, D), dtype=jnp.float32), 'W1': jax.random.normal(ks[2], (E, D, F), dtype=jnp.float32) * s_in, 'b1': jnp.zeros((E, F), dtype=jnp.float32), 'W2': jax.random.normal(ks[3], (E, F, D), dtype=jnp.float32) * s_mid, 'b2': jnp.zeros((E, D), dtype=jnp.float32)}
    _L0_ffn_in = _L0_ffn_setup()
    _d = {'L0_attn_x': _L0_attn_in['x'], 'L0_attn_W_q': _L0_attn_in['W_q'], 'L0_attn_W_k': _L0_attn_in['W_k'], 'L0_attn_W_v': _L0_attn_in['W_v'], 'L0_attn_W_o': _L0_attn_in['W_o'], 'L0_ffn_Wg': _L0_ffn_in['Wg'], 'L0_ffn_gamma': _L0_ffn_in['gamma'], 'L0_ffn_beta': _L0_ffn_in['beta'], 'L0_ffn_W1': _L0_ffn_in['W1'], 'L0_ffn_b1': _L0_ffn_in['b1'], 'L0_ffn_W2': _L0_ffn_in['W2'], 'L0_ffn_b2': _L0_ffn_in['b2']}
    _x0 = _d['L0_attn_x']
    _d['L0_attn_x'] = jax.random.normal(jax.random.fold_in(jax.random.key(seed), 1), (4, 1024, 128), dtype=_x0.dtype)
    del _x0
    return _d

def reference(L0_attn_x, L0_attn_W_q, L0_attn_W_k, L0_attn_W_v, L0_attn_W_o, L0_ffn_Wg, L0_ffn_gamma, L0_ffn_beta, L0_ffn_W1, L0_ffn_b1, L0_ffn_W2, L0_ffn_b2):

    def _L0_attn_ref(x, W_q, W_k, W_v, W_o):
        import jax, jax.numpy as jnp
        import numpy as np
        B, S, D, H = (4, 256, 128, 16)
        DK = D // H

        def apply_rope(x, pos, inv_freq):
            sincos = pos[:, :, None].astype(jnp.float32) * inv_freq
            sin = jnp.repeat(jnp.sin(sincos), 2, axis=-1)[:, None]
            cos = jnp.repeat(jnp.cos(sincos), 2, axis=-1)[:, None]
            x_rot = jnp.stack([-x[..., 1::2], x[..., ::2]], axis=-1).reshape(x.shape)
            return x * cos + x_rot * sin
        b, s, _ = x.shape
        pos = jnp.arange(s)[None, :]
        inv_freq = 1.0 / 10000.0 ** (jnp.arange(0, DK, 2, dtype=jnp.float32) / DK)

        def proj(W):
            return (x @ W.T).reshape(b, s, H, DK).transpose(0, 2, 1, 3)
        Q = apply_rope(proj(W_q), pos, inv_freq)
        K = apply_rope(proj(W_k), pos, inv_freq)
        V = proj(W_v)
        scores = jnp.einsum('bhqd,bhkd->bhqk', Q, K) / jnp.sqrt(jnp.float32(DK))
        attn = jax.nn.softmax(scores, axis=-1)
        out = jnp.einsum('bhqk,bhkd->bhqd', attn, V)
        out = out.transpose(0, 2, 1, 3).reshape(b, s, D)
        return out @ W_o.T

    def _L0_ffn_ref(x, Wg, gamma, beta, W1, b1, W2, b2):
        import jax, jax.numpy as jnp
        import numpy as np
        E, K, D, F = (8, 2, 128, 512)
        EPS = 1e-06
        B, S = (2, 128)
        orig_shape = x.shape
        xf = x.reshape(-1, orig_shape[-1])
        scores = xf @ Wg
        w, idx = jax.lax.top_k(scores, K)
        w = jax.nn.softmax(w, axis=-1)
        mu = jnp.mean(xf, axis=-1, keepdims=True)
        var = jnp.var(xf, axis=-1, keepdims=True)
        xhat = (xf - mu) * jax.lax.rsqrt(var + EPS)
        normed = xhat[None, :, :] * gamma[:, None, :] + beta[:, None, :]
        h = jax.nn.relu(jnp.einsum('end,edf->enf', normed, W1) + b1[:, None, :])
        out = jnp.einsum('enf,efd->end', h, W2) + b2[:, None, :] + xf[None, :, :]
        cw = jnp.sum(w[..., None] * jax.nn.one_hot(idx, E, dtype=w.dtype), axis=1)
        y = jnp.einsum('ne,end->nd', cw, out)
        return y.reshape(orig_shape)
    x = L0_attn_x
    xn = _layernorm(x, axis=-1)
    x = x + _L0_attn_ref(xn, L0_attn_W_q, L0_attn_W_k, L0_attn_W_v, L0_attn_W_o) + _L0_ffn_ref(xn, L0_ffn_Wg, L0_ffn_gamma, L0_ffn_beta, L0_ffn_W1, L0_ffn_b1, L0_ffn_W2, L0_ffn_b2)
    return x

_drawn_inputs = setup_inputs


def setup_inputs(seed=0):
    import zlib

    import numpy as np

    out = dict(_drawn_inputs(seed))
    spreads = {'L0_ffn_gamma': (1.0, 0.2),
     'L0_ffn_beta': (0.0, 0.316),
     'L0_ffn_b1': (0.0, 0.319),
     'L0_ffn_b2': (0.0, 0.1)}
    factors = {}
    for name, (base, spread) in spreads.items():
        noise = np.random.default_rng([zlib.crc32(name.encode()), seed]).standard_normal(out[name].shape)
        drawn = base * np.exp(spread * noise) if base else spread * noise
        out[name] = jnp.asarray(drawn.astype(out[name].dtype))
    for name, factor in factors.items():
        out[name] = (out[name] * factor).astype(out[name].dtype)
    return out
```

```python
import math
from contextlib import ExitStack

import numpy as np
import concourse.bass as bass
from concourse import mybir

F32 = mybir.dt.float32
BF16 = mybir.dt.bfloat16
I32 = mybir.dt.int32
U32 = mybir.dt.uint32
ALU = mybir.AluOpType
ACT = mybir.ActivationFunctionType
AX = mybir.AxisListType

P = 128
B, S, D = 4, 1024, 128
H, DK = 16, 8
E, F = 8, 512
T = B * S // P
TB = S // P
CH = 512
PAIRS = B * H // 2
PB = PAIRS // B
PARTS = 3
ROWS = PARTS * PARTS * DK
KR = ROWS + PARTS
LOADS = 2 * PARTS * PARTS
KB = S // P
FC = F // P
SLOT_TILES = 72
BODY = 6
W_LEN = F + F + FC + 2 + D
W2_AT, B1_AT, GA_AT, BE_AT, B2_AT = F, 2 * F, 2 * F + FC, 2 * F + FC + 1, 2 * F + FC + 2
SCALE = 1.0 / math.sqrt(DK)
SAFE = 60.0
MID = 8
ITERS = PAIRS // 2


def build(nc, x_d, wq_d, wk_d, wv_d, wo_d, wg_d, gamma_d, beta_d, w1_d, b1_d, w2_d, b2_d, cos_d, sin_d, const_d,
          out_d):
    ctx = ExitStack()
    with ctx:
        def sb(name, shape, dt=F32):
            return ctx.enter_context(nc.sbuf_tensor(name, shape, dt))

        def sem(name):
            return ctx.enter_context(nc.semaphore(name))

        parts_d = [nc.dram_tensor(f"parts_{s}", [PARTS, PAIRS, 2 * DK, S], BF16, kind="Internal").ap()
                   for s in "qk"]
        xs_d = nc.dram_tensor("slot_in", [(SLOT_TILES + 1) * P, D], F32, kind="Internal").ap()
        ys_d = nc.dram_tensor("slot_out", [SLOT_TILES * P, D], F32, kind="Internal").ap()

        x = sb("x", [P, T, D])
        xn = sb("xn", [P, T, D])
        xh = sb("xh", [P, T, D])
        xnT = sb("xnT", [P, T * P])
        att = xnT[:, :].rearrange("p (b q w) -> p b q w", b=B, q=TB)
        v_all = sb("v_all", [P, PAIRS, KB, 2 * DK])
        ring = sb("ring", [P, 8, CH])
        prod_c = [ring[:, k, :] for k in range(4)]
        prod_s = [ring[:, 4 + k, :] for k in range(4)]
        probs = [ring[:, 2 * k:2 * k + 2, :] for k in range(4)]
        work = sb("work", [P, 3 * PARTS * CH // 2])
        part = work[:, :].bitcast(BF16).rearrange("p (k i c) -> p k i c", k=3, i=PARTS)
        tables = sb("tables", [P, 3 * W_LEN])
        cos, sin = tables[:, 0:S], tables[:, S:2 * S]
        const = sb("const", [P, 4 * P])
        ident, before = const[:, 0:P], const[:, P:2 * P]
        head_row = const[:, 2 * P:2 * P + 32]
        iota_e, iota_t = const[:, 3 * P:3 * P + E], const[:, 3 * P + E:3 * P + E + SLOT_TILES + 1]
        ones = sb("ones", [P, P])
        wr = sb("wr", [P, 4, D])
        wT = sb("wT", [P, 4, D])
        wvg = sb("wvg", [P, D + E])
        woT = sb("woT", [P, D])
        rows = sb("rows", [P, D])
        w_all = sb("w_all", [P, E, W_LEN])
        w_tile = [tables[:, k * W_LEN:(k + 1) * W_LEN] for k in range(3)]
        qs = [sb(f"qs{k}", [P, 2, S], BF16) for k in range(2)]
        ks = [sb(f"ks{k}", [P, 2, S], BF16) for k in range(2)]
        v_aug = [sb(f"v_aug{k}", [P, KB, 2, 32]) for k in range(2)]
        rank_words = wr[:, :, :].rearrange("p k d -> p (k d)")
        acc_s = sb("acc_s", [P, CH])
        rec = sb("rec", [P, 4, 4])
        stats = sb("stats", [P, T, 6])
        mv = sb("mv", [P, T, 2])
        small = sb("small", [P, 12, T])
        score = sb("score", [P, T, E])
        top = sb("top", [P, T, 8])
        topi = sb("topi", [P, T, 8], U32)
        topf = sb("topf", [P, T, 2])
        pick = sb("pick", [P, 2, T, E])
        cnt = sb("cnt", [P, 4, T, E])
        rank = rank_words[:, :].rearrange("p (a t e) -> p a t e", a=2, e=E)
        exp_s = sb("exp_s", [P, 4, E])
        exp_i = sb("exp_i", [P, 2, E], I32)
        slot_f = sb("slot_f", [P, 2, T])
        slot = sb("slot", [P, 2, T], U32)
        owner_f = sb("owner_f", [1, 2, SLOT_TILES + 1])
        owner = sb("owner", [1, SLOT_TILES + 1], I32)
        head_of = sb("head_of", [P, 32], BF16)
        square = [sb(f"square{k}", [P, CH], BF16) for k in range(2)]
        norms = sb("norms", [P, B])
        norm_b = sb("norm_b", [B, 3, H])
        norm_m = sb("norm_m", [B, 1])
        flag_f = sb("flag_f", [1, 2, 1])
        flag = sb("flag", [1, 1], I32)
        tiles = [work[:, k * P:(k + 1) * P] for k in range(3 * PARTS * CH // 2 // P)]
        xt, xsT, ys, oT, fin = tiles[0:3], tiles[3:5], tiles[5:7], tiles[7:9], tiles[0:4]
        hT = [work[:, (9 + FC * k) * P:(9 + FC * (k + 1)) * P].rearrange("p (c n) -> p c n", c=FC) for k in range(2)]
        mx = sb("mx", [P, 2 * TB])
        mrow = sb("mrow", [2 * TB, 3, P])
        mpart = sb("mpart", [2 * TB, PARTS, P], BF16)

        sc = [ctx.enter_context(nc.psum_tensor(f"sc{k}", [P, 2 * CH], F32)) for k in range(3)]
        acc = [ctx.enter_context(nc.psum_tensor(f"acc{k}", [P, CH], F32)) for k in range(2)]

        x_in = [sem(f"x_in{b}") for b in range(B)]
        w_in, rows_in, const_in, rope_in, gate_in, exp_in = (
            sem(n) for n in ("w_in", "rows_in", "const_in", "rope_in", "gate_in", "exp_in"))
        zeroed, scattered, gathered = sem("zeroed"), sem("scattered"), sem("gathered")
        stack_ok, slots_zero, v_zero, v_one, dve, ln_var, ln_sqrt, xn_ok, xh_ok = (sem(n) for n in
                                                      ("stack_ok", "slots_zero", "v_zero", "v_one", "dve", "ln_var", "ln_sqrt", "xn_ok", "xh_ok"))
        wtr, wtr_out, rtr, rtr_out = sem("wtr"), sem("wtr_out"), sem("rtr"), sem("rtr_out")
        xtr, xtr_out, proj, rope_out, v_mm, v_out = (sem(n) for n in
                                                     ("xtr", "xtr_out", "proj", "rope_out", "v_mm", "v_out"))
        rope_sum, hi_ok, mid_in, mid_ok, lo_ok = (sem(n) for n in
                                                            ("rope_sum", "hi_ok", "mid_in", "mid_ok", "lo_ok"))
        part_out = [sem(f"part_out{k}") for k in range(3)]
        gap_ok, gate_exp, pick_ok, rank_mm, rank_ok, slot_ok, owner_ok = (sem(n) for n in
                                                                 ("gap_ok", "gate_exp", "pick_ok", "rank_mm", "rank_ok",
                                                                  "slot_ok", "owner_ok"))
        sq_ok, norm_mm, norm_in, bound_tr, bound_ok, bound_tr2, flag_ok, head_ok = (
            sem(n) for n in ("sq_ok", "norm_mm", "norm_in", "bound_tr", "bound_ok", "bound_tr2", "flag_ok",
                             "head_ok"))
        base_ok = sem("base_ok")
        qk_in = [sem(f"qk_in{k}") for k in range(2)]
        v_ok, s_mm, e_ok, pv_mm, acc_ok, acc_tr, norm_ok = (sem(n) for n in
                                                                   ("v_ok", "s_mm", "e_ok", "pv_mm",
                                                                    "acc_ok", "acc_tr", "norm_ok"))
        m_mm, m_red, m_tr, m_split, m_in, m_chain, m_seen, rec_ok = (sem(n) for n in
                                                           ("m_mm", "m_red", "m_tr", "m_split", "m_in", "m_chain", "m_seen",
                                                            "rec_ok"))
        xt_tr, xsT_ok, w_ok, h_mm, relu_ok, y_mm, y_ok = (sem(n) for n in
                                                                        ("xt_tr", "xsT_ok", "w_ok", "h_mm",
                                                                         "relu_ok", "y_mm", "y_ok"))
        xt_in = [sem(f"xt_in{k}") for k in range(3)]
        y_out = [sem(f"y_out{k}") for k in range(2)]
        fin_out = [sem(f"fin_out{k}") for k in range(4)]
        o_tr, oT_ok, o_mm, fin_ok = (sem(n) for n in ("o_tr", "oT_ok", "o_mm", "fin_ok"))

        block = ctx.enter_context(nc.Block())

        def wait(eng, s, value):
            if not isinstance(value, int) or value > 0:
                eng.wait_ge(s, value)

        def steps():
            return [(4 * b + 2 * c + s, b, c, s) for b in range(B) for c in range(2) for s in range(2)]

        def token_tile(batch, half, c):
            return batch * TB + half * (TB // 2) + c

        @block.sync
        def _(sp):
            for b in range(B):
                sp.dma_start(x[:, b * TB:(b + 1) * TB, :],
                             x_d[b].rearrange("(t p) d -> p t d", p=P)).then_inc(x_in[b], 16)
            sp.dma_start(cos, cos_d).then_inc(rope_in, 16)
            sp.dma_start(sin, sin_d).then_inc(rope_in, 16)
            for e in range(E):
                sp.dma_start(w_all[:, e, 0:F], w1_d[e]).then_inc(exp_in, 16)
                sp.dma_start(w_all[:, e, W2_AT:W2_AT + F].rearrange("p (c d) -> p c d", c=FC),
                             w2_d[e].rearrange("(c p) d -> p c d", p=P)).then_inc(exp_in, 16)
                sp.dma_start(w_all[:, e, B2_AT:B2_AT + D], b2_d[e:e + 1, :].to_broadcast([P, D])).then_inc(exp_in, 16)

            for n, b, c, s in steps():
                sp.wait_ge(lo_ok, n + 1)
                for i in range(PARTS):
                    dst = parts_d[s][i, b * PB:(b + 1) * PB, :, c * CH:(c + 1) * CH]
                    sp.dma_start(dst.rearrange("a r t -> (a r) t"), part[:, n % 3, i, :]).then_inc(part_out[n % 3], 16)

            def load_pair(p, k):
                wait(sp, s_mm, 16 * (p - 1))
                for side, dst in ((0, qs[k]), (1, ks[k])):
                    for i in range(PARTS):
                        for j in range(PARTS):
                            r = (PARTS * i + j) * DK
                            src = parts_d[side][(i, j)[side], bass.ds(p, 1), :, :]
                            src = src.rearrange("o (a d) t -> (o d) a t", a=2)
                            sp.dma_start(dst[r:r + DK, :, :], src).then_inc(qk_in[k], 16)

            for k in range(3):
                sp.wait_ge(part_out[k], 16 * PARTS * len(steps()[k::3]))
            sp.wait_ge(stack_ok, 1)
            load_pair(0, 0)
            load_pair(1, 1)
            with sp.Fori(1, MID + 1) as i:
                load_pair(2 * i, 0)
                load_pair(2 * i + 1, 1)

            def tile_io(i, j):
                t = BODY * i + j
                wait(sp, xt_tr, t)
                sp.dma_start(xt[(j + 2) % 3], xs_d[bass.ds((t + 2) * P, P), :]).then_inc(xt_in[(j + 2) % 3], 16)

            def tile_store(i, j):
                t = BODY * i + j
                sp.wait_ge(y_ok, t + 1)
                sp.dma_start(ys_d[bass.ds(t * P, P), :], ys[j % 2]).then_inc(y_out[j % 2], 16)

            sp.wait_ge(scattered, 16 * 2 * T)
            for t in range(2):
                sp.dma_start(xt[t], xs_d[t * P:(t + 1) * P, :]).then_inc(xt_in[t], 16)
            for j in range(BODY):
                tile_io(0, j)
                if j > 0:
                    tile_store(0, j - 1)
            with sp.Fori(1, SLOT_TILES // BODY - 1) as i:
                for j in range(BODY):
                    tile_io(i, j)
                    if j > 0:
                        tile_store(i, j - 1)
                    else:
                        tile_store(i - 1, BODY - 1)
            last = SLOT_TILES // BODY - 1
            for j in range(BODY):
                if BODY * last + j + 2 <= SLOT_TILES:
                    tile_io(last, j)
                if j > 0:
                    tile_store(last, j - 1)
                else:
                    tile_store(last - 1, BODY - 1)
            tile_store(last, BODY - 1)

            with sp.Fori(MID + 1, ITERS) as i:
                load_pair(2 * i, 0)
                load_pair(2 * i + 1, 1)

            for t in range(T):
                sp.wait_ge(fin_ok, t + 1)
                sp.dma_start(out_d[t // TB, (t % TB) * P:(t % TB + 1) * P, :], fin[t % 4]).then_inc(fin_out[t % 4], 16)
            for k in range(4):
                sp.wait_ge(fin_out[k], 16 * T // 4)

        @block.gpsimd
        def _(pool):
            nc.gpsimd.memset(xh[:, :, :], 0.0).then_inc(slots_zero, 1)
            pool.wait_ge(slots_zero, 1)
            for t in range(0, SLOT_TILES + 1, T):
                n = min(T, SLOT_TILES + 1 - t)
                pool.dma_start(xs_d[t * P:(t + n) * P, :].rearrange("(t p) d -> p t d", p=P),
                               xh[:, 0:n, :]).then_inc(zeroed, 16)
            for k in range(2):
                v = v_aug[k]
                nc.gpsimd.memset(v[:, :, :, :], 0.0).then_inc(v_zero, 1)
            pool.wait_ge(v_zero, 2)
            for k in range(2):
                nc.gpsimd.memset(v_aug[k][:, :, :, DK:DK + 1], 1.0).then_inc(v_one, 1)
            for n, b, c, s in steps():
                pool.wait_ge(rope_out, 2 * (n + 1))
                nc.gpsimd.tensor_tensor(prod_c[n % 4], prod_c[n % 4], prod_s[n % 4], ALU.add).then_inc(rope_sum, 1)
            pool.wait_ge(xn_ok, T)
            pool.wait_ge(zeroed, 48)
            for t in range(T):
                nc.gpsimd.tensor_scalar(xh[:, t, :], xn[:, t, :], small[:, 7, t:t + 1], None,
                                        ALU.mult).then_inc(xh_ok, 1)

            pool.wait_ge(slot_ok, 2)
            pool.wait_ge(xh_ok, T)
            for t in range(T):
                for k in range(2):
                    pool.indirect_dma_start(out=xs_d[:, :],
                                            out_offset=bass.IndirectOffsetOnAxis(ap=slot[:, k, t:t + 1], axis=0),
                                            in_=xh[:, t, :], in_offset=None).then_inc(scattered, 16)

            pool.wait_ge(flag_ok, 1)
            fast = pool.value_load(flag[0:1, 0:1], min_val=0, max_val=1)

            def pair_io(p, k):
                with pool.If(fast == 0):
                    pool.wait_ge(m_split, p + 1)
                    pool.sem_inc(m_seen)
                    for i in range(PARTS):
                        pool.dma_start(qs[k][ROWS + i:ROWS + i + 1, :, :].rearrange("o a (q c) -> o (a q) c", c=P),
                                       mpart[:, i, :]).then_inc(m_in, 16)

            pair_io(0, 0)
            pair_io(1, 1)
            with pool.Fori(1, MID + 1) as i:
                pair_io(2 * i, 0)
                pair_io(2 * i + 1, 1)
            for k in range(2):
                pool.wait_ge(y_out[k], 16 * SLOT_TILES // 2)
            pool.wait_ge(base_ok, T)
            for t in range(T):
                for k, dst in ((0, xn), (1, xh)):
                    pool.indirect_dma_start(out=dst[:, t, :], out_offset=None, in_=ys_d[:, :],
                                            in_offset=bass.IndirectOffsetOnAxis(ap=slot[:, k, t:t + 1], axis=0)
                                            ).then_inc(gathered, 16)
            with pool.Fori(MID + 1, ITERS) as i:
                pair_io(2 * i, 0)
                pair_io(2 * i + 1, 1)

        @block.tensor
        def _(pe):
            pe.wait_ge(const_in, 16)
            pe.wait_ge(w_in, 64)
            for k in range(4):
                last = nc.tensor.transpose(sc[0][:, k * D:(k + 1) * D], wr[:, k, :], ident)
            last.then_inc(wtr, 1)
            pe.wait_ge(rows_in, 48)
            nc.tensor.transpose(sc[0][:, CH:CH + 48], rows[0:48, :], ident[0:48, 0:48]).then_inc(rtr, 1)

            def head_norms(n):
                b, c, s = n // 4, n // 2 % 2, n % 2
                pe.wait_ge(sq_ok, n + 1)
                wait(pe, norm_in, b)
                j = 32 * (2 * s + c)
                nc.tensor.matmul(acc[1][j:j + 32, :], head_of[:, :], square[s][:, :], start=True,
                                 stop=True).then_inc(norm_mm, 1)

            pe.wait_ge(head_ok, 1)
            pe.wait_ge(wtr_out, 6)
            pe.wait_ge(rtr_out, 3)
            pe.wait_ge(gate_in, 16)
            for b in range(B):
                pe.wait_ge(xn_ok, TB * (b + 1))
                wait(pe, xtr_out, b)
                for t in range(TB):
                    last = nc.tensor.transpose(sc[2][:, t * P:(t + 1) * P], xn[:, b * TB + t, :], ident)
                last.then_inc(xtr, 1)
                pe.wait_ge(xtr_out, b + 1)
                for c in range(2):
                    src = xnT[:, b * S + c * CH:b * S + (c + 1) * CH]
                    for s in range(2):
                        n = 4 * b + 2 * c + s
                        wait(pe, rope_out, 2 * (n - 1))
                        for r in range(2):
                            last = nc.tensor.matmul(sc[s][:, r * CH:(r + 1) * CH], wT[:, 2 * s + r, :], src,
                                                    start=True, stop=True)
                        last.then_inc(proj, 1)
                    for g in range(2):
                        q = 4 * b + 2 * c + g
                        if q > 0:
                            head_norms(q - 1)
                        wait(pe, v_out, 8 * q)
                        for u in range(2):
                            t = 2 * q + u
                            last = nc.tensor.matmul(acc[0][:, u * (D + E):(u + 1) * (D + E)],
                                                    xnT[:, t * P:(t + 1) * P], wvg[:, :], start=True, stop=True)
                        last.then_inc(v_mm, 1)
            head_norms(4 * B - 1)

            pe.wait_ge(norm_in, B)
            nc.tensor.transpose(acc[1][0:B, 0:P], norms[:, :], ident).then_inc(bound_tr, 1)
            pe.wait_ge(bound_ok, 1)
            nc.tensor.transpose(acc[1][0:1, P:P + B], norm_m[:, :], ident[0:B, 0:B]).then_inc(bound_tr2, 1)
            pe.wait_ge(flag_ok, 1)
            fast = pe.value_load(flag[0:1, 0:1], min_val=0, max_val=1)

            def scores(k, u, a, kb):
                for half in range(2):
                    last = nc.tensor.matmul(sc[u][:, half * CH:(half + 1) * CH], ks[k][0:KR, a, kb * P:(kb + 1) * P],
                                            qs[k][0:KR, a, half * CH:(half + 1) * CH], start=True, stop=True)
                last.then_inc(s_mm, 1)

            def maxima(p, k):
                wait(pe, e_ok, 16 * p)
                for n in range(2 * TB):
                    a, q = n // TB, n % TB
                    if n >= 2:
                        pe.wait_ge(m_red, 16 * p + n - 1)
                    for half in range(2):
                        last = nc.tensor.matmul(sc[n % 2][:, half * CH:(half + 1) * CH],
                                                qs[k][0:ROWS, a, q * P:(q + 1) * P],
                                                ks[k][0:ROWS, a, half * CH:(half + 1) * CH], start=True, stop=True)
                    last.then_inc(m_mm, 1)
                pe.wait_ge(m_red, 16 * (p + 1))
                nc.tensor.transpose(sc[2][0:2 * TB, 0:P], mx[:, :], ident).then_inc(m_tr, 1)
                pe.wait_ge(m_in, 48 * (p + 1))

            def enter_pair(i, k):
                p = 2 * i + k
                pe.wait_ge(qk_in[k], 16 * LOADS * (i + 1))
                with pe.If(fast == 0):
                    maxima(p, k)

            def untangle(p, k):
                pe.wait_ge(acc_ok, p + 1)
                for c in range(4):
                    last = nc.tensor.transpose(acc[k][:, c * P:(c + 1) * P], acc_s[:, c * P:(c + 1) * P], ident)
                last.then_inc(acc_tr, 1)

            def ranks():
                pe.wait_ge(pick_ok, 1)
                nc.tensor.matmul(acc[1][:, 0:T * E], before, cnt[:, 0, :, :], start=True, stop=True)
                nc.tensor.matmul(acc[1][:, T * E:2 * T * E], ones[:, :], cnt[:, 0, :, :], start=True,
                                 stop=True).then_inc(rank_mm, 1)
                pe.wait_ge(rank_ok, 1)

            def attend(i, first, last_iter):
                for s in range(2 * KB):
                    k, kb = s // KB, s % KB
                    p = 2 * i + k
                    if s + 1 < 2 * KB or not last_iter:
                        nk, nkb = ((s + 1) // KB) % 2, (s + 1) % KB
                        if nkb == 0:
                            enter_pair(i + (s + 1) // (2 * KB), nk)
                        for a in range(2):
                            u = 2 * (s + 1) + a
                            if s + 1 == 2 * KB:
                                pe.wait_ge(e_ok, 32 * i + 31 + a)
                                scores(nk, a, a, nkb)
                            else:
                                if u >= 3:
                                    pe.wait_ge(e_ok, 32 * i + u - 2)
                                scores(nk, u % 3, a, nkb)
                    if kb == 0:
                        if first and k == 1:
                            ranks()
                        pe.wait_ge(v_ok, p + 1)
                        if not (first and k == 0):
                            wait(pe, norm_ok, p - 1)
                    pe.wait_ge(e_ok, 32 * i + 2 * s + 2)
                    for a in range(2):
                        for half in range(2):
                            j = 2 * a + half
                            mm = nc.tensor.matmul(acc[k][32 * j:32 * j + 32, :], v_aug[k][:, kb, a, :],
                                                  probs[(2 * s + a) % 4][:, half, :],
                                                  start=(kb == 0), stop=(kb == KB - 1))
                    mm.then_inc(pv_mm, 1)
                    if kb == 1 and not (first and k == 0):
                        untangle(p - 1, 1 - k)

            enter_pair(0, 0)
            for a in range(2):
                scores(0, a, a, 0)
            attend(0, True, False)
            with pe.Fori(1, MID) as i:
                attend(i, False, False)

            def tile_in(i, j):
                pe.wait_ge(xt_in[j % 3], 16 * (BODY // 3 * i + j // 3 + 1))
                nc.tensor.transpose(sc[2][:, (j % 2) * CH:(j % 2) * CH + P], xt[j % 3], ident).then_inc(xt_tr, 1)

            def layer_one(t, j):
                pe.wait_ge(xsT_ok, t + 1)
                for c in range(FC):
                    mm = nc.tensor.matmul(sc[0][:, (j % 2) * CH + c * P:(j % 2) * CH + (c + 1) * P],
                                          w_tile[j % 3][:, c * P:(c + 1) * P], xsT[j % 2],
                                          start=True, stop=True)
                mm.then_inc(h_mm, 1)

            def layer_two(t, j):
                pe.wait_ge(relu_ok, t + 1)
                wait(pe, y_ok, t - 1)
                for c in range(FC):
                    mm = nc.tensor.matmul(sc[1][:, (j % 2) * CH:(j % 2) * CH + D], hT[j % 2][:, c, :],
                                          w_tile[j % 3][:, W2_AT + c * D:W2_AT + (c + 1) * D],
                                          start=(c == 0), stop=(c == FC - 1))
                mm.then_inc(y_mm, 1)

            def expert_body(i, first):
                for j in range(BODY):
                    t = BODY * i + j
                    tile_in(i, j + 1)
                    layer_one(t, j)
                    if not (first and j == 0):
                        layer_two(t - 1, j + BODY - 1)

            pe.wait_ge(e_ok, 32 * MID + 2)
            tile_in(0, 0)
            expert_body(0, True)
            with pe.Fori(1, SLOT_TILES // BODY) as i:
                expert_body(i, False)
            layer_two(SLOT_TILES - 1, BODY - 1)

            pe.wait_ge(y_ok, SLOT_TILES)
            pe.wait_ge(xsT_ok, SLOT_TILES + 1)
            with pe.Fori(MID, ITERS - 1) as i:
                attend(i, False, False)
            attend(ITERS - 1, False, True)
            untangle(PAIRS - 1, 1)

            pe.wait_ge(norm_ok, PAIRS)
            for t in range(T):
                b, q = t // TB, t % TB
                wait(pe, oT_ok, t - 1)
                nc.tensor.transpose(sc[0][:, (t % 2) * CH:(t % 2) * CH + P], att[:, b, q, :],
                                    ident).then_inc(o_tr, 1)
                if t > 0:
                    project(pe, t - 1, sc, oT, woT, oT_ok, fin_ok, o_mm, nc, wait)
            project(pe, T - 1, sc, oT, woT, oT_ok, fin_ok, o_mm, nc, wait)

        @block.scalar
        def _(act):
            act.dma_start(const[:, :], const_d).then_inc(const_in, 16)
            for k, w in enumerate((wq_d, wk_d, wv_d, wo_d)):
                act.dma_start(wr[:, k, :], w).then_inc(w_in, 16)
            act.dma_start(rows[0:32, :], b1_d.rearrange("e (c p) -> (e c) p", p=P)).then_inc(rows_in, 16)
            act.dma_start(rows[32:40, :], gamma_d).then_inc(rows_in, 16)
            act.dma_start(rows[40:48, :], beta_d).then_inc(rows_in, 16)
            act.dma_start(wvg[:, D:D + E], wg_d).then_inc(gate_in, 16)

            for k in range(2):
                act.wait_ge(ln_var, k + 1)
                nc.scalar.activation(small[:, 9 + k, :], small[:, 3 + 2 * k, :], ACT.Sqrt).then_inc(ln_sqrt, 1)

            def high(n):
                act.wait_ge(rope_sum, n + 1)
                wait(act, part_out[n % 3], 16 * PARTS * (n // 3))
                nc.scalar.copy(part[:, n % 3, 0, :], prod_c[n % 4]).then_inc(hi_ok, 1)

            def squares(n):
                wait(act, norm_mm, n - 1)
                nc.scalar.activation(square[n % 2][:, :], prod_c[n % 4], ACT.Square).then_inc(sq_ok, 1)

            def middle(n):
                act.wait_ge(mid_in, n + 1)
                nc.scalar.copy(part[:, n % 3, 1, :], prod_c[n % 4]).then_inc(mid_ok, 1)

            def columns(b):
                act.wait_ge(xtr, b + 1)
                nc.scalar.copy(xnT[:, b * S:(b + 1) * S], sc[2][:, :]).then_inc(xtr_out, 1)

            columns(0)
            for b in range(B):
                for c in range(2):
                    for g in range(2):
                        n = 4 * b + 2 * c + g
                        high(n)
                        squares(n)
                        q = n
                        act.wait_ge(v_mm, q + 1)
                        for u in range(2):
                            t = 2 * q + u
                            src = acc[0][:, u * (D + E):(u + 1) * (D + E)]
                            nc.scalar.copy(v_all[:, b * PB:(b + 1) * PB, t % TB, :],
                                           src[:, 0:D].rearrange("p (a w) -> p a w", a=PB)).then_inc(v_out, 2)
                            nc.scalar.copy(score[:, t, :], src[:, D:D + E]).then_inc(v_out, 2)
                        if c == 1 and g == 1 and b + 1 < B:
                            columns(b + 1)
                        middle(n)

            def attend(i):
                for u in range(4 * KB):
                    s = u // 2
                    act.wait_ge(s_mm, 32 * i + u + 1)
                    if u % 2 == 0:
                        wait(act, pv_mm, 16 * i + s - 1)
                    nc.scalar.activation(probs[u % 4], sc[u % 32 % 3][:, :].rearrange("p (h c) -> p h c", h=2),
                                         ACT.Exp, scale=SCALE).then_inc(e_ok, 1)
                    if u == 2 * KB - 1 and isinstance(i, int):
                        act.wait_ge(gap_ok, 1)
                        nc.scalar.activation(small[:, 1, :], small[:, 0, :], ACT.Exp).then_inc(gate_exp, 1)

            act.wait_ge(flag_ok, 1)
            attend(0)
            with act.Fori(1, MID) as i:
                attend(i)

            def exp_unit(i, u):
                act.wait_ge(s_mm, 32 * i + u + 1)
                if u % 2 == 0:
                    wait(act, pv_mm, 16 * i + u // 2 - 1)
                nc.scalar.activation(probs[u % 4], sc[u % 3][:, :].rearrange("p (h c) -> p h c", h=2),
                                     ACT.Exp, scale=SCALE).then_inc(e_ok, 1)

            exp_unit(MID, 0)
            exp_unit(MID, 1)

            def relu(i, j):
                t = BODY * i + j
                act.wait_ge(h_mm, t + 1)
                wait(act, y_mm, t - 1)
                for c in range(FC):
                    a = nc.scalar.activation(hT[j % 2][:, c, :], sc[0][:, (j % 2) * CH + c * P:
                                                                       (j % 2) * CH + (c + 1) * P],
                                             ACT.Relu, bias=w_tile[j % 3][:, B1_AT + c:B1_AT + c + 1])
                a.then_inc(relu_ok, 1)

            for j in range(BODY):
                relu(0, j)
            with act.Fori(1, SLOT_TILES // BODY) as i:
                for j in range(BODY):
                    relu(i, j)

            for u in range(2, 4 * KB):
                exp_unit(MID, u)
            with act.Fori(MID + 1, ITERS) as i:
                attend(i)

            for t in range(T):
                act.wait_ge(o_tr, t + 1)
                wait(act, o_mm, t - 1)
                nc.scalar.copy(oT[t % 2], sc[0][:, (t % 2) * CH:(t % 2) * CH + P]).then_inc(oT_ok, 1)

        @block.vector
        def _(v):
            chain = [0]

            def link(ins):
                chain[0] += 1
                ins.then_inc(dve, 1)
                v.wait_ge(dve, chain[0])

            nc.vector.memset(ones[:, :], 1.0)
            for k in range(2):
                nc.vector.memset(qs[k][64:96, :, :], 0.0)
                last = nc.vector.memset(ks[k][64:96, :, :], 1.0)
            last.then_inc(stack_ok, 1)

            for b in range(B):
                v.wait_ge(x_in[b], 16)
                for t in range(b * TB, (b + 1) * TB):
                    last = nc.vector.bn_stats(stats[:, t, :], x[:, t, :])
            link(last)
            for t in range(T):
                last = nc.vector.bn_aggr(mv[:, t, :], stats[:, t, :])
            link(last)
            mean, var = mv[:, :, 0], mv[:, :, 1]

            def inverse_root(k, dst):
                val, rec_ = small[:, 2 + 2 * k, :], small[:, 3 + 2 * k, :]
                nc.vector.reciprocal(rec_, val).then_inc(ln_var, 1)
                y0, tmp, y = small[:, 9 + k, :], small[:, 11, :], small[:, dst, :]
                v.wait_ge(ln_sqrt, k + 1)
                link(nc.vector.tensor_tensor(tmp, y0, y0, ALU.mult))
                link(nc.vector.tensor_tensor(tmp, tmp, val, ALU.mult))
                link(nc.vector.tensor_scalar(tmp, tmp, -0.5, 1.5, ALU.mult, ALU.add))
                link(nc.vector.tensor_tensor(y, y0, tmp, ALU.mult))

            link(nc.vector.tensor_scalar(small[:, 2, :], var, 1e-5, None, ALU.add))
            inverse_root(0, 6)
            rstd = small[:, 6, :]
            link(nc.vector.tensor_tensor(small[:, 4, :], var, rstd, ALU.mult))
            link(nc.vector.tensor_tensor(small[:, 4, :], small[:, 4, :], rstd, ALU.mult))
            link(nc.vector.tensor_scalar(small[:, 4, :], small[:, 4, :], 1e-6, None, ALU.add))
            inverse_root(1, 7)
            link(nc.vector.tensor_tensor(small[:, 8, :], mean, rstd, ALU.mult))
            for t in range(T):
                nc.vector.tensor_scalar(xn[:, t, :], x[:, t, :], small[:, 6, t:t + 1], small[:, 8, t:t + 1],
                                        ALU.mult, ALU.subtract).then_inc(xn_ok, 1)

            v.wait_ge(wtr, 1)
            ps = sc[0][:, 0:4 * D].rearrange("p (k d) -> p k d", k=4)
            for s in range(2):
                nc.vector.tensor_copy(wT[:, 2 * s, :], ps[:, s, :]).then_inc(wtr_out, 1)
                two = ps[:, s, :].rearrange("p (i r) -> p i r", r=2)
                rot = wT[:, 2 * s + 1, :].rearrange("p (i r) -> p i r", r=2)
                nc.vector.tensor_scalar(rot[:, :, 0], two[:, :, 1], -1.0, None, ALU.mult)
                nc.vector.tensor_copy(rot[:, :, 1], two[:, :, 0]).then_inc(wtr_out, 1)
            nc.vector.tensor_copy(wvg[:, 0:D], ps[:, 2, :]).then_inc(wtr_out, 1)
            nc.vector.tensor_copy(woT[:, :], ps[:, 3, :]).then_inc(wtr_out, 1)
            v.wait_ge(rtr, 1)
            nc.vector.tensor_copy(w_all[:, :, B1_AT:B1_AT + FC],
                                  sc[0][:, CH:CH + 32].rearrange("p (e c) -> p e c", e=E)).then_inc(rtr_out, 1)
            nc.vector.tensor_copy(w_all[:, :, GA_AT], sc[0][:, CH + 32:CH + 40]).then_inc(rtr_out, 1)
            nc.vector.tensor_copy(w_all[:, :, BE_AT], sc[0][:, CH + 40:CH + 48]).then_inc(rtr_out, 1)

            v.wait_ge(rope_in, 32)
            nc.vector.tensor_copy(head_of[:, :], head_row).then_inc(head_ok, 1)

            def rotate(n, c, s):
                v.wait_ge(proj, n + 1)
                wait(v, lo_ok, n - 3)
                pos = slice(c * CH, (c + 1) * CH)
                nc.vector.tensor_tensor(prod_c[n % 4], sc[s][:, 0:CH], cos[:, pos], ALU.mult).then_inc(rope_out, 1)
                nc.vector.tensor_tensor(prod_s[n % 4], sc[s][:, CH:2 * CH], sin[:, pos], ALU.mult
                                        ).then_inc(rope_out, 1)

            def rest_one(n, b, c, s):
                v.wait_ge(rope_sum, n + 1)
                v.wait_ge(hi_ok, n + 1)
                v.wait_ge(sq_ok, n + 1)
                nc.vector.tensor_tensor(prod_c[n % 4], prod_c[n % 4], part[:, n % 3, 0, :], ALU.subtract
                                        ).then_inc(mid_in, 1)

            def rest_two(n):
                v.wait_ge(mid_ok, n + 1)
                nc.vector.tensor_tensor(part[:, n % 3, 2, :], prod_c[n % 4], part[:, n % 3, 1, :], ALU.subtract
                                        ).then_inc(lo_ok, 1)

            order = steps()
            def batch_norms(b):
                v.wait_ge(norm_mm, 4 * (b + 1))
                nc.vector.reduce_max(norms[:, b:b + 1], acc[1][:, :], AX.X).then_inc(norm_in, 1)

            for n, b, c, s in order:
                if n % 4 == 1 and b > 0:
                    batch_norms(b - 1)
                rotate(n, c, s)
                if n >= 1:
                    rest_one(*order[n - 1])
                if n >= 2:
                    rest_two(n - 2)
            rest_one(*order[-1])
            rest_two(len(order) - 2)
            rest_two(len(order) - 1)
            batch_norms(B - 1)

            v.wait_ge(bound_tr, 1)
            rows4 = acc[1][0:B, 0:P].rearrange("b (s c h) -> b s c h", s=2, c=2)
            for k in range(2):
                link(nc.vector.reduce_max(norm_b[:, k, :], rows4[:, k, :, 0:H].rearrange("b c h -> b h c"), AX.X))
            link(nc.vector.tensor_tensor(norm_b[:, 2, :], norm_b[:, 0, :], norm_b[:, 1, :], ALU.mult))
            nc.vector.reduce_max(norm_m[:, :], norm_b[:, 2, :], AX.X).then_inc(bound_ok, 1)
            v.wait_ge(bound_tr2, 1)
            link(nc.vector.reduce_max(flag_f[:, 0, :], acc[1][0:1, P:P + B], AX.X))
            link(nc.vector.tensor_scalar(flag_f[:, 1, :], flag_f[:, 0, :], (SAFE / SCALE) ** 2, None, ALU.is_le))
            nc.vector.tensor_copy(flag[:, :], flag_f[:, 1, :]).then_inc(flag_ok, 1)

            v.wait_ge(flag_ok, 1)
            fast = v.value_load(flag[0:1, 0:1], min_val=0, max_val=1)

            def maxima(p):
                for n in range(2 * TB):
                    v.wait_ge(m_mm, 16 * p + n + 1)
                    nc.vector.reduce_max(mx[:, n:n + 1], sc[n % 2][:, :], AX.X).then_inc(m_red, 1)
                v.wait_ge(m_tr, p + 1)
                wait(v, m_in, 48 * p)
                base = 5 * p
                nc.vector.tensor_scalar(mrow[:, 0, :], sc[2][0:2 * TB, 0:P], -1.0, None, ALU.mult).then_inc(m_chain, 1)
                v.wait_ge(m_chain, base + 1)
                nc.vector.tensor_copy(mpart[:, 0, :], mrow[:, 0, :]).then_inc(m_chain, 1)
                v.wait_ge(m_chain, base + 2)
                nc.vector.tensor_tensor(mrow[:, 1, :], mrow[:, 0, :], mpart[:, 0, :], ALU.subtract
                                        ).then_inc(m_chain, 1)
                v.wait_ge(m_chain, base + 3)
                nc.vector.tensor_copy(mpart[:, 1, :], mrow[:, 1, :]).then_inc(m_chain, 1)
                v.wait_ge(m_chain, base + 4)
                nc.vector.tensor_tensor(mrow[:, 2, :], mrow[:, 1, :], mpart[:, 1, :], ALU.subtract
                                        ).then_inc(m_chain, 1)
                v.wait_ge(m_chain, base + 5)
                nc.vector.tensor_copy(mpart[:, 2, :], mrow[:, 2, :]).then_inc(m_split, 1)

            def normalise(p, k):
                v.wait_ge(acc_tr, p + 1)
                ps = acc[k][:, :].rearrange("p (c a h w) -> p c a h w", c=4, a=2, h=2)
                for a in range(2):
                    nc.vector.reciprocal(rec[:, 2 * a:2 * a + 2, :], ps[:, :, a, :, DK].rearrange("p c h -> p h c")
                                         ).then_inc(rec_ok, 1)
                v.wait_ge(rec_ok, 2 * (p + 1))
                for a in range(2):
                    for h in range(2):
                        dst = att[:, bass.ds(p // PB, 1), 4 * h:4 * h + 4,
                                  bass.ds((p % PB) * 2 * DK + a * DK, DK)]
                        m = nc.vector.tensor_tensor(dst.rearrange("p o c d -> p (o c) d"), ps[:, :, a, h, 0:DK],
                                                    rec[:, 2 * a + h, :].unsqueeze(2).to_broadcast([P, 4, DK]),
                                                    ALU.mult)
                m.then_inc(norm_ok, 1)

            def take(p, k):
                v.wait_ge(pv_mm, 8 * (p + 1))
                nc.vector.tensor_copy(acc_s[:, :], acc[k][:, :]).then_inc(acc_ok, 1)

            def route():
                for t in range(T):
                    last = nc.vector.max(top[:, t, :], score[:, t, :])
                link(last)
                for t in range(T):
                    last = nc.vector.max_index(topi[:, t, :], top[:, t, :], score[:, t, :])
                link(last)
                nc.vector.tensor_tensor(small[:, 0, :], top[:, :, 1], top[:, :, 0], ALU.subtract).then_inc(gap_ok, 1)
                link(nc.vector.tensor_copy(topf[:, :, :], topi[:, :, 0:2]))
                for k in range(2):
                    link(nc.vector.tensor_tensor(pick[:, k, :, :], iota_e.unsqueeze(1).to_broadcast([P, T, E]),
                                                 topf[:, :, k:k + 1].to_broadcast([P, T, E]), ALU.is_equal))
                nc.vector.tensor_tensor(cnt[:, 0, :, :], pick[:, 0, :, :], pick[:, 1, :, :], ALU.add
                                        ).then_inc(pick_ok, 1)

            def take_ranks():
                v.wait_ge(rank_mm, 1)
                nc.vector.tensor_copy(rank[:, :, :, :], acc[1][:, :].rearrange("p (a t e) -> p a t e", a=2, e=E)
                                      ).then_inc(rank_ok, 1)

            def place():
                v.wait_ge(gate_exp, 1)
                e, w1, w2, ws = small[:, 1, :], small[:, 2, :], small[:, 3, :], small[:, 4, :]
                link(nc.vector.tensor_scalar(w2, e, 1.0, None, ALU.add))
                link(nc.vector.reciprocal(w1, w2))
                link(nc.vector.tensor_tensor(w2, e, w1, ALU.mult))
                link(nc.vector.tensor_tensor(ws, w1, w2, ALU.add))

                v.wait_ge(rank_ok, 1)
                link(nc.vector.tensor_copy(cnt[:, 1, :, :], rank[:, 1, :, :]))
                a, shift = 1, 1
                while shift < T:
                    nxt = 3 - a
                    nc.vector.tensor_copy(cnt[:, nxt, 0:shift, :], cnt[:, a, 0:shift, :])
                    link(nc.vector.tensor_tensor(cnt[:, nxt, shift:T, :], cnt[:, a, shift:T, :],
                                                 cnt[:, a, 0:T - shift, :], ALU.add))
                    a, shift = nxt, 2 * shift
                incl = cnt[:, a, :, :]
                total = incl[:, T - 1, :]
                link(nc.vector.tensor_scalar(exp_s[:, 0, :], total, float(P - 1), None, ALU.add))
                link(nc.vector.tensor_copy(exp_i[:, 0, :], exp_s[:, 0, :]))
                link(nc.vector.tensor_scalar(exp_i[:, 1, :], exp_i[:, 0, :], 7, None, ALU.arith_shift_right))
                link(nc.vector.tensor_copy(exp_s[:, 0, :], exp_i[:, 1, :]))
                link(nc.vector.tensor_copy(exp_s[:, 1, :], exp_s[:, 0, :]))
                a2, shift = 1, 1
                while shift < E:
                    nxt = 3 - a2
                    nc.vector.tensor_copy(exp_s[:, nxt, 0:shift], exp_s[:, a2, 0:shift])
                    link(nc.vector.tensor_tensor(exp_s[:, nxt, shift:E], exp_s[:, a2, shift:E],
                                                 exp_s[:, a2, 0:E - shift], ALU.add))
                    a2, shift = nxt, 2 * shift
                ends = exp_s[:, a2, :]
                link(nc.vector.tensor_tensor(exp_s[:, 3, :], ends, exp_s[:, 0, :], ALU.subtract))
                link(nc.vector.tensor_scalar(exp_s[:, 3, :], exp_s[:, 3, :], float(P), None, ALU.mult))
                pos = cnt[:, 3, :, :]
                link(nc.vector.tensor_tensor(pos, incl, rank[:, 1, :, :],
                                             ALU.subtract))
                link(nc.vector.tensor_tensor(pos, pos, rank[:, 0, :, :], ALU.add))
                link(nc.vector.tensor_tensor(pos, pos, exp_s[:, 3:4, :].to_broadcast([P, T, E]), ALU.add))
                for k in range(2):
                    link(nc.vector.tensor_tensor(cnt[:, 0, :, :], pos, pick[:, k, :, :], ALU.mult))
                    link(nc.vector.reduce_sum(slot_f[:, k, :], cnt[:, 0, :, :], AX.X))
                    nc.vector.tensor_copy(slot[:, k, :], slot_f[:, k, :]).then_inc(slot_ok, 1)
                own_cmp = cnt[0:1, :, :, :].rearrange("p a t e -> p (a t) e")[:, 0:SLOT_TILES + 1, :]
                link(nc.vector.tensor_tensor(own_cmp,
                                             iota_t[0:1, :].unsqueeze(2).to_broadcast([1, SLOT_TILES + 1, E]),
                                             exp_s[0:1, a2:a2 + 1, :].to_broadcast([1, SLOT_TILES + 1, E]), ALU.is_ge))
                link(nc.vector.reduce_sum(owner_f[:, 0, :], own_cmp, AX.X))
                link(nc.vector.tensor_scalar(owner_f[:, 1, :], owner_f[:, 0, :], float(E - 1), None, ALU.min))
                nc.vector.tensor_copy(owner[:, :], owner_f[:, 1, :]).then_inc(owner_ok, 1)


            def residuals():
                v.wait_ge(xh_ok, T)
                for t in range(T):
                    nc.vector.scalar_tensor_tensor(out=x[:, t, :], in0=xn[:, t, :], scalar=small[:, 4, t:t + 1],
                                                   in1=x[:, t, :], op0=ALU.mult, op1=ALU.add).then_inc(base_ok, 1)

            def copy_v(p, k):
                wait(v, pv_mm, 8 * (p - 1))
                nc.vector.tensor_copy(v_aug[k][:, :, :, 0:DK],
                                      v_all[:, bass.ds(p, 1), :, :].rearrange("p o k (a d) -> p (o k) a d", a=2)
                                      ).then_inc(v_ok, 1)

            def attend(i, last_iter, before_take, after_take):
                for k in range(2):
                    p = 2 * i + k
                    if not isinstance(p, int) or p > 0:
                        normalise(p - 1, 1 - k)
                    if not (last_iter and k == 1):
                        copy_v(p + 1, 1 - k)
                    if before_take[k]:
                        before_take[k]()
                    if not (last_iter and k == 1):
                        with v.If(fast == 0):
                            maxima(p + 1)
                    take(p, k)
                    if after_take[k]:
                        after_take[k]()

            with v.If(fast == 0):
                maxima(0)
            nothing = (None, None)
            v.wait_ge(v_one, 2)
            v.wait_ge(v_out, 4 * T)
            copy_v(0, 0)
            attend(0, False, (route, None), (take_ranks, place))
            attend(1, False, nothing, (residuals, None))
            with v.Fori(2, MID) as i:
                attend(i, False, nothing, nothing)

            v.wait_ge(exp_in, 16 * 3 * E)

            def weights(t, j):
                e = v.value_load(owner[0:1, bass.ds(t, 1)], min_val=0, max_val=E - 1)
                wait(v, y_ok, t - 2)
                nc.vector.tensor_copy(w_tile[j % 3],
                                      w_all[:, bass.ds(e, 1), :].rearrange("p o w -> p (o w)")).then_inc(w_ok, 1)

            def columns(t, j):
                v.wait_ge(xt_tr, t + 1)
                v.wait_ge(w_ok, t + 1)
                wait(v, h_mm, t - 1)
                nc.vector.tensor_scalar(xsT[j % 2], sc[2][:, (j % 2) * CH:(j % 2) * CH + P],
                                        w_tile[j % 3][:, GA_AT:GA_AT + 1], w_tile[j % 3][:, BE_AT:BE_AT + 1],
                                        ALU.mult, ALU.add).then_inc(xsT_ok, 1)

            def rows_out(i, j):
                t = BODY * i + j
                v.wait_ge(y_mm, t + 1)
                wait(v, y_out[j % 2], 16 * (BODY // 2 * i + j // 2))
                nc.vector.tensor_tensor(ys[j % 2], sc[1][:, (j % 2) * CH:(j % 2) * CH + D],
                                        w_tile[j % 3][:, B2_AT:B2_AT + D], ALU.add).then_inc(y_ok, 1)

            def expert_body(i, first):
                for j in range(BODY):
                    t = BODY * i + j
                    weights(t + 1, j + 1)
                    columns(t + 1, j + 1)
                    if not (first and j == 0):
                        rows_out(i, j - 1)

            weights(0, 0)
            columns(0, 0)
            expert_body(0, True)
            with v.Fori(1, SLOT_TILES // BODY) as i:
                expert_body(i, False)
            rows_out(SLOT_TILES // BODY - 1, BODY - 1)

            with v.Fori(MID, ITERS - 1) as i:
                attend(i, False, nothing, nothing)
            attend(ITERS - 1, True, nothing, nothing)
            normalise(PAIRS - 1, 1)

            for t in range(T):
                v.wait_ge(gathered, 16 * 2 * T)
                link(nc.vector.scalar_tensor_tensor(out=x[:, t, :], in0=xn[:, t, :], scalar=small[:, 2, t:t + 1],
                                                    in1=x[:, t, :], op0=ALU.mult, op1=ALU.add))
                link(nc.vector.scalar_tensor_tensor(out=x[:, t, :], in0=xh[:, t, :], scalar=small[:, 3, t:t + 1],
                                                    in1=x[:, t, :], op0=ALU.mult, op1=ALU.add))
                v.wait_ge(o_mm, t + 1)
                wait(v, fin_out[t % 4], 16 * (t // 4))
                nc.vector.tensor_tensor(fin[t % 4], sc[1][:, (t % 2) * CH:(t % 2) * CH + D], x[:, t, :],
                                        ALU.add).then_inc(fin_ok, 1)


def project(pe, t, sc, oT, woT, oT_ok, fin_ok, o_mm, nc, wait):
    pe.wait_ge(oT_ok, t + 1)
    wait(pe, fin_ok, t - 1)
    nc.tensor.matmul(sc[1][:, (t % 2) * CH:(t % 2) * CH + D], oT[t % 2], woT[:, :], start=True,
                     stop=True).then_inc(o_mm, 1)


def rope_tables():
    inv_freq = (np.float32(1.0) / np.power(np.float32(10000.0), np.arange(0, DK, 2, dtype=np.float32)
                                           / np.float32(DK))).astype(np.float32)
    angle = np.arange(S, dtype=np.float32)[None, :] * np.tile(np.repeat(inv_freq, 2), H)[:, None]
    return np.cos(angle).astype(np.float32), np.sin(angle).astype(np.float32)


def constants():
    c = np.zeros((P, 4 * P), np.float32)
    i = np.arange(P)
    c[:, 0:P] = np.eye(P)
    c[:, P:2 * P] = i[:, None] < i[None, :]
    c[:, 2 * P:2 * P + H] = (i[:, None] // DK) == np.arange(H)[None, :]
    c[:, 3 * P:3 * P + E] = np.arange(E)
    c[:, 3 * P + E:3 * P + E + SLOT_TILES + 1] = np.arange(SLOT_TILES + 1)
    return c


INPUTS = ["L0_attn_x", "L0_attn_W_q", "L0_attn_W_k", "L0_attn_W_v", "L0_attn_W_o", "L0_ffn_Wg", "L0_ffn_gamma",
          "L0_ffn_beta", "L0_ffn_W1", "L0_ffn_b1", "L0_ffn_W2", "L0_ffn_b2"]


def kernel(**inputs):
    import concourse.bacc as bacc
    from concourse.bass_utils import run_bass_kernel_spmd

    nc = bacc.Bacc("TRN2", target_bir_lowering=False, num_devices=1)
    arrays, args = {}, []
    cos, sin = rope_tables()
    given = [(n, np.ascontiguousarray(inputs[n])) for n in INPUTS]
    given += [("rope_cos", cos), ("rope_sin", sin), ("shape_constants", constants())]
    for name, a in given:
        arrays[name] = a
        args.append(nc.dram_tensor(name, a.shape, mybir.dt.from_np(a.dtype), kind="ExternalInput").ap())
    args.append(nc.dram_tensor("out", (B, S, D), F32, kind="ExternalOutput").ap())
    build(nc, *args)
    return run_bass_kernel_spmd(nc, [arrays], core_ids=[0]).results[0]["out"]
```

```python
import math
from contextlib import ExitStack

import numpy as np
import concourse.bass as bass
from concourse import mybir

F32 = mybir.dt.float32
BF16 = mybir.dt.bfloat16
I32 = mybir.dt.int32
U32 = mybir.dt.uint32
ALU = mybir.AluOpType
ACT = mybir.ActivationFunctionType
AX = mybir.AxisListType

P = 128
B, S, D = 4, 1024, 128
H, DK = 16, 8
E, F = 8, 512
T = B * S // P
TB = S // P
CH = 512
PAIRS = B * H // 2
PB = PAIRS // B
PARTS = 3
ROWS = PARTS * PARTS * DK
KR = ROWS + PARTS
LOADS = 2 * PARTS * PARTS
KB = S // P
FC = F // P
SLOT_TILES = 72
BODY = 8
XS_TILES = SLOT_TILES + 3
W_LEN = F + F + FC + 2 + D
W2_AT, B1_AT, GA_AT, BE_AT, B2_AT = F, 2 * F, 2 * F + FC, 2 * F + FC + 1, 2 * F + FC + 2
SCALE = 1.0 / math.sqrt(DK)
SAFE = 60.0
MID = 4
ITERS = PAIRS // 2
MERGE = (11, 15)
G = 4


def build(nc, x_d, wq_d, wk_d, wv_d, wo_d, wg_d, gamma_d, beta_d, w1_d, b1_d, w2_d, b2_d, cos_d, sin_d, const_d,
          out_d):
    ctx = ExitStack()
    with ctx:
        def sb(name, shape, dt=F32):
            return ctx.enter_context(nc.sbuf_tensor(name, shape, dt))

        def sem(name):
            return ctx.enter_context(nc.semaphore(name))

        parts_d = [nc.dram_tensor(f"parts_{s}", [PARTS, PAIRS, 2 * DK, S], BF16, kind="Internal").ap()
                   for s in "qk"]
        xs_d = nc.dram_tensor("slot_in", [XS_TILES * P, D], F32, kind="Internal").ap()
        ys_d = nc.dram_tensor("slot_out", [SLOT_TILES * P, D], F32, kind="Internal").ap()

        x = sb("x", [P, T, D])
        xn = sb("xn", [P, T, D])
        xh = sb("xh", [P, T, D])
        xnT = sb("xnT", [P, T * P])
        att = xnT[:, :].rearrange("p (b q w) -> p b q w", b=B, q=TB)
        v_all = sb("v_all", [P, PAIRS, KB, 2 * DK])
        ring = sb("ring", [P, 8, CH])
        prod_c = [ring[:, k, :] for k in range(4)]
        prod_s = [ring[:, 4 + k, :] for k in range(4)]
        probs = [ring[:, 2 * k:2 * k + 2, :] for k in range(4)]
        work = sb("work", [P, 3 * PARTS * CH // 2])
        part = work[:, :].bitcast(BF16).rearrange("p (k i c) -> p k i c", k=3, i=PARTS)
        tables = sb("tables", [P, 3 * W_LEN])
        cos, sin = tables[:, 0:S], tables[:, S:2 * S]
        const = sb("const", [P, 4 * P])
        ident, before = const[:, 0:P], const[:, P:2 * P]
        head_row = const[:, 2 * P:2 * P + 32]
        iota_e, iota_t = const[:, 3 * P:3 * P + E], const[:, 3 * P + E:3 * P + E + SLOT_TILES + 2]
        early = sb("early", [P, 10 * D])
        wr = early[:, 0:4 * D].rearrange("p (k d) -> p k d", k=4)
        wT = early[:, 4 * D:8 * D].rearrange("p (k d) -> p k d", k=4)
        ones, rows = early[:, 8 * D:9 * D], early[:, 9 * D:10 * D]
        wvg = sb("wvg", [P, D + E])
        woT = sb("woT", [P, D])
        w_all = sb("w_all", [P, E, W_LEN])
        w_tile = [tables[:, k * W_LEN:(k + 1) * W_LEN] for k in range(3)] + [early[:, 0:W_LEN]]
        qs = [sb(f"qs{k}", [P, 2, S], BF16) for k in range(2)]
        ks = [sb(f"ks{k}", [P, 2, S], BF16) for k in range(2)]
        v_aug = [sb(f"v_aug{k}", [P, KB, 2, 32]) for k in range(2)]
        rank_words = early[:, 0:4 * D]
        acc_s = sb("acc_s", [P, CH])
        rec = sb("rec", [P, 4, 4])
        stats = sb("stats", [P, T, 6])
        mv = sb("mv", [P, T, 2])
        small = sb("small", [P, 12, T])
        score = sb("score", [P, T, E])
        top = sb("top", [P, T, 8])
        topi = sb("topi", [P, T, 8], U32)
        topf = sb("topf", [P, T, 2])
        pick = sb("pick", [P, 2, T, E])
        cnt = sb("cnt", [P, 4, T, E])
        rank = rank_words[:, :].rearrange("p (a t e) -> p a t e", a=2, e=E)
        exp_s = sb("exp_s", [P, 4, E])
        exp_i = sb("exp_i", [P, 2, E], I32)
        slot_f = sb("slot_f", [P, 2, T])
        slot = sb("slot", [P, 2, T], U32)
        owner_f = sb("owner_f", [1, 2, SLOT_TILES + 2])
        owner = sb("owner", [1, SLOT_TILES + 2], I32)
        head_of = sb("head_of", [P, 32], BF16)
        square = [sb(f"square{k}", [P, CH], BF16) for k in range(2)]
        norms = sb("norms", [P, B])
        norm_b = sb("norm_b", [B, 3, H])
        norm_m = sb("norm_m", [B, 1])
        flag_f = sb("flag_f", [1, 2, 1])
        flag = sb("flag", [1, 1], I32)
        tiles = [work[:, k * P:(k + 1) * P] for k in range(3 * PARTS * CH // 2 // P)]
        xt, xsT, ys = tiles[0:4], tiles[4:6], tiles[6:8]
        hT = [work[:, (8 + FC * k) * P:(8 + FC * (k + 1)) * P].rearrange("p (c n) -> p c n", c=FC) for k in range(2)]
        oT, fin = ([work[:, (k + n) * G * P:(k + n + 1) * G * P].rearrange("p (t c) -> p t c", t=G)
                    for n in range(2)] for k in (0, 2))
        mx = sb("mx", [P, 2 * TB])
        mrow = sb("mrow", [2 * TB, 3, P])
        mpart = sb("mpart", [2 * TB, PARTS, P], BF16)

        sc = [ctx.enter_context(nc.psum_tensor(f"sc{k}", [P, 2 * CH], F32)) for k in range(3)]
        acc = [ctx.enter_context(nc.psum_tensor(f"acc{k}", [P, CH], F32)) for k in range(2)]

        x_in = [sem(f"x_in{b}") for b in range(B)]
        w_in, rows_in, const_in, rope_in, gate_in, exp_in = (
            sem(n) for n in ("w_in", "rows_in", "const_in", "rope_in", "gate_in", "exp_in"))
        zeroed, scattered, gathered = sem("zeroed"), sem("scattered"), sem("gathered")
        stack_ok, slots_zero, v_zero, v_one, dve, ln_var, ln_sqrt, xn_ok, xh_ok = (sem(n) for n in
                                                      ("stack_ok", "slots_zero", "v_zero", "v_one", "dve", "ln_var", "ln_sqrt", "xn_ok", "xh_ok"))
        wtr, wtr_out, rtr, rtr_out = sem("wtr"), sem("wtr_out"), sem("rtr"), sem("rtr_out")
        xtr, xtr_out, proj, rope_out, v_mm, v_out = (sem(n) for n in
                                                     ("xtr", "xtr_out", "proj", "rope_out", "v_mm", "v_out"))
        rope_sum, hi_ok, mid_in, mid_ok, lo_ok = (sem(n) for n in
                                                            ("rope_sum", "hi_ok", "mid_in", "mid_ok", "lo_ok"))
        part_out = [sem(f"part_out{k}") for k in range(3)]
        gap_ok, gate_exp, pick_ok, rank_mm, rank_ok, slot_ok, owner_ok = (sem(n) for n in
                                                                 ("gap_ok", "gate_exp", "pick_ok", "rank_mm", "rank_ok",
                                                                  "slot_ok", "owner_ok"))
        sq_ok, norm_mm, norm_in, bound_tr, bound_ok, bound_tr2, flag_ok, head_ok = (
            sem(n) for n in ("sq_ok", "norm_mm", "norm_in", "bound_tr", "bound_ok", "bound_tr2", "flag_ok",
                             "head_ok"))
        base_ok = sem("base_ok")
        qk_in = [sem(f"qk_in{k}") for k in range(2)]
        v_ok, s_mm, e_ok, pv_mm, acc_ok, acc_tr, norm_ok = (sem(n) for n in
                                                                   ("v_ok", "s_mm", "e_ok", "pv_mm",
                                                                    "acc_ok", "acc_tr", "norm_ok"))
        m_mm, m_red, m_tr, m_split, m_in, m_chain, rec_ok = (sem(n) for n in
                                                           ("m_mm", "m_red", "m_tr", "m_split", "m_in", "m_chain",
                                                            "rec_ok"))
        xt_tr, xsT_ok, w_ok, h_mm, relu_ok, y_mm, y_ok = (sem(n) for n in
                                                                        ("xt_tr", "xsT_ok", "w_ok", "h_mm",
                                                                         "relu_ok", "y_mm", "y_ok"))
        xt_in = [sem(f"xt_in{k}") for k in range(4)]
        y_out = [sem(f"y_out{k}") for k in range(2)]
        fin_out = [sem(f"fin_out{k}") for k in range(2)]
        o_tr, oT_ok, o_mm, fin_ok = (sem(n) for n in ("o_tr", "oT_ok", "o_mm", "fin_ok"))

        block = ctx.enter_context(nc.Block())

        def wait(eng, s, value):
            if not isinstance(value, int) or value > 0:
                eng.wait_ge(s, value)

        def steps():
            return [(4 * b + 2 * c + s, b, c, s) for b in range(B) for c in range(2) for s in range(2)]

        def token_tile(batch, half, c):
            return batch * TB + half * (TB // 2) + c

        @block.sync
        def _(sp):
            for b in range(B):
                sp.dma_start(x[:, b * TB:(b + 1) * TB, :],
                             x_d[b].rearrange("(t p) d -> p t d", p=P)).then_inc(x_in[b], 16)
            sp.dma_start(cos, cos_d).then_inc(rope_in, 16)
            sp.dma_start(sin, sin_d).then_inc(rope_in, 16)
            for e in range(E):
                sp.dma_start(w_all[:, e, 0:F], w1_d[e]).then_inc(exp_in, 16)
                sp.dma_start(w_all[:, e, W2_AT:W2_AT + F].rearrange("p (c d) -> p c d", c=FC),
                             w2_d[e].rearrange("(c p) d -> p c d", p=P)).then_inc(exp_in, 16)
                sp.dma_start(w_all[:, e, B2_AT:B2_AT + D], b2_d[e:e + 1, :].to_broadcast([P, D])).then_inc(exp_in, 16)

            for n, b, c, s in steps():
                sp.wait_ge(lo_ok, n + 1)
                for i in range(PARTS):
                    dst = parts_d[s][i, b * PB:(b + 1) * PB, :, c * CH:(c + 1) * CH]
                    sp.dma_start(dst.rearrange("a r t -> (a r) t"), part[:, n % 3, i, :]).then_inc(part_out[n % 3], 16)

            def load_pair(p, k):
                wait(sp, s_mm, 16 * (p - 1))
                for side, dst in ((0, qs[k]), (1, ks[k])):
                    for i in range(PARTS):
                        for j in range(PARTS):
                            r = (PARTS * i + j) * DK
                            src = parts_d[side][(i, j)[side], bass.ds(p, 1), :, :]
                            src = src.rearrange("o (a d) t -> (o d) a t", a=2)
                            sp.dma_start(dst[r:r + DK, :, :], src).then_inc(qk_in[k], 16)

            for k in range(3):
                sp.wait_ge(part_out[k], 16 * PARTS * len(steps()[k::3]))
            sp.wait_ge(stack_ok, 1)
            load_pair(0, 0)
            load_pair(1, 1)
            sp.wait_ge(flag_ok, 1)
            fast = sp.value_load(flag[0:1, 0:1], min_val=0, max_val=1)

            def store_max(p, k):
                with sp.If(fast == 0):
                    sp.wait_ge(m_split, p + 1)
                    for i in range(PARTS):
                        sp.dma_start(qs[k][ROWS + i:ROWS + i + 1, :, :].rearrange("o a (q c) -> o (a q) c", c=P),
                                     mpart[:, i, :]).then_inc(m_in, 16)

            def feed(i):
                load_pair(2 * i, 0)
                store_max(2 * i - 1, 1)
                load_pair(2 * i + 1, 1)
                store_max(2 * i, 0)

            store_max(0, 0)
            with sp.Fori(1, MID + 1) as i:
                feed(i)

            def tile_load(i, j):
                t = BODY * i + j
                wait(sp, xt_tr, t)
                sp.dma_start(xt[(j + 3) % 4], xs_d[bass.ds((t + 3) * P, P), :]).then_inc(xt_in[(j + 3) % 4], 16)

            def tile_store(i, j):
                t = BODY * i + j
                sp.wait_ge(y_ok, t + 1)
                sp.dma_start(ys_d[bass.ds(t * P, P), :], ys[j % 2]).then_inc(y_out[j % 2], 16)

            def expert_io(i, first):
                for j in range(BODY):
                    tile_load(i, j)
                    if not (first and j < 3):
                        tile_store(i, j - 3)

            sp.wait_ge(scattered, 16 * 2 * T)
            for t in range(3):
                sp.dma_start(xt[t], xs_d[t * P:(t + 1) * P, :]).then_inc(xt_in[t], 16)
            expert_io(0, True)
            with sp.Fori(1, SLOT_TILES // BODY) as i:
                expert_io(i, False)
            for j in range(3):
                tile_store(SLOT_TILES // BODY, j - 3)

            with sp.Fori(MID + 1, ITERS) as i:
                feed(i)
            store_max(PAIRS - 1, 1)

            for g in range(T // G):
                sp.wait_ge(fin_ok, g + 1)
                b, t = g * G // TB, g * G % TB
                sp.dma_start(out_d[b, t * P:(t + G) * P, :].rearrange("(t p) d -> p t d", p=P),
                             fin[g % 2]).then_inc(fin_out[g % 2], 16)
            for k in range(2):
                sp.wait_ge(fin_out[k], 16 * T // G // 2)

        @block.gpsimd
        def _(pool):
            nc.gpsimd.memset(xh[:, :, :], 0.0).then_inc(slots_zero, 1)
            pool.wait_ge(slots_zero, 1)
            for t in range(0, XS_TILES, T):
                n = min(T, XS_TILES - t)
                pool.dma_start(xs_d[t * P:(t + n) * P, :].rearrange("(t p) d -> p t d", p=P),
                               xh[:, 0:n, :]).then_inc(zeroed, 16)
            for k in range(2):
                v = v_aug[k]
                nc.gpsimd.memset(v[:, :, :, :], 0.0).then_inc(v_zero, 1)
            pool.wait_ge(v_zero, 2)
            for k in range(2):
                nc.gpsimd.memset(v_aug[k][:, :, :, DK:DK + 1], 1.0).then_inc(v_one, 1)
            for n, b, c, s in steps():
                pool.wait_ge(rope_out, 2 * (n + 1))
                nc.gpsimd.tensor_tensor(prod_c[n % 4], prod_c[n % 4], prod_s[n % 4], ALU.add).then_inc(rope_sum, 1)
            pool.wait_ge(xn_ok, T)
            pool.wait_ge(zeroed, 48)
            for t in range(T):
                nc.gpsimd.tensor_scalar(xh[:, t, :], xn[:, t, :], small[:, 7, t:t + 1], None,
                                        ALU.mult).then_inc(xh_ok, 1)

            pool.wait_ge(slot_ok, 2)
            pool.wait_ge(xh_ok, T)
            for t in range(T):
                for k in range(2):
                    pool.indirect_dma_start(out=xs_d[:, :],
                                            out_offset=bass.IndirectOffsetOnAxis(ap=slot[:, k, t:t + 1], axis=0),
                                            in_=xh[:, t, :], in_offset=None).then_inc(scattered, 16)

            for k in range(2):
                pool.wait_ge(y_out[k], 16 * SLOT_TILES // 2)
            pool.wait_ge(base_ok, T)
            for t in range(T):
                for k, dst in ((0, xn), (1, xh)):
                    pool.indirect_dma_start(out=dst[:, t, :], out_offset=None, in_=ys_d[:, :],
                                            in_offset=bass.IndirectOffsetOnAxis(ap=slot[:, k, t:t + 1], axis=0)
                                            ).then_inc(gathered, 16)

        @block.tensor
        def _(pe):
            pe.wait_ge(const_in, 16)
            pe.wait_ge(w_in, 64)
            for k in range(4):
                last = nc.tensor.transpose(sc[0][:, k * D:(k + 1) * D], wr[:, k, :], ident)
            last.then_inc(wtr, 1)
            pe.wait_ge(rows_in, 48)
            nc.tensor.transpose(sc[0][:, CH:CH + 48], rows[0:48, :], ident[0:48, 0:48]).then_inc(rtr, 1)

            def head_norms(n):
                b, c, s = n // 4, n // 2 % 2, n % 2
                pe.wait_ge(sq_ok, n + 1)
                wait(pe, norm_in, b)
                j = 32 * (2 * s + c)
                nc.tensor.matmul(acc[1][j:j + 32, :], head_of[:, :], square[s][:, :], start=True,
                                 stop=True).then_inc(norm_mm, 1)

            pe.wait_ge(head_ok, 1)
            pe.wait_ge(wtr_out, 6)
            pe.wait_ge(rtr_out, 3)
            pe.wait_ge(gate_in, 16)
            for b in range(B):
                pe.wait_ge(xn_ok, TB * (b + 1))
                wait(pe, xtr_out, b)
                for t in range(TB):
                    last = nc.tensor.transpose(sc[2][:, t * P:(t + 1) * P], xn[:, b * TB + t, :], ident)
                last.then_inc(xtr, 1)
                pe.wait_ge(xtr_out, b + 1)
                for c in range(2):
                    src = xnT[:, b * S + c * CH:b * S + (c + 1) * CH]
                    for s in range(2):
                        n = 4 * b + 2 * c + s
                        wait(pe, rope_out, 2 * (n - 1))
                        for r in range(2):
                            last = nc.tensor.matmul(sc[s][:, r * CH:(r + 1) * CH], wT[:, 2 * s + r, :], src,
                                                    start=True, stop=True)
                        last.then_inc(proj, 1)
                    for g in range(2):
                        q = 4 * b + 2 * c + g
                        if q > 0:
                            head_norms(q - 1)
                        wait(pe, v_out, 8 * q)
                        for u in range(2):
                            t = 2 * q + u
                            last = nc.tensor.matmul(acc[0][:, u * (D + E):(u + 1) * (D + E)],
                                                    xnT[:, t * P:(t + 1) * P], wvg[:, :], start=True, stop=True)
                        last.then_inc(v_mm, 1)
            head_norms(4 * B - 1)

            pe.wait_ge(norm_in, B)
            nc.tensor.transpose(acc[1][0:B, 0:P], norms[:, :], ident).then_inc(bound_tr, 1)
            pe.wait_ge(bound_ok, 1)
            nc.tensor.transpose(acc[1][0:1, P:P + B], norm_m[:, :], ident[0:B, 0:B]).then_inc(bound_tr2, 1)
            pe.wait_ge(flag_ok, 1)
            fast = pe.value_load(flag[0:1, 0:1], min_val=0, max_val=1)

            def scores(k, u, a, kb):
                for half in range(2):
                    last = nc.tensor.matmul(sc[u][:, half * CH:(half + 1) * CH], ks[k][0:KR, a, kb * P:(kb + 1) * P],
                                            qs[k][0:KR, a, half * CH:(half + 1) * CH], start=True, stop=True)
                last.then_inc(s_mm, 1)

            def maxima(p, k):
                wait(pe, e_ok, 16 * p)
                for n in range(2 * TB):
                    a, q = n // TB, n % TB
                    if n >= 2:
                        pe.wait_ge(m_red, 16 * p + n - 1)
                    for half in range(2):
                        last = nc.tensor.matmul(sc[n % 2][:, half * CH:(half + 1) * CH],
                                                qs[k][0:ROWS, a, q * P:(q + 1) * P],
                                                ks[k][0:ROWS, a, half * CH:(half + 1) * CH], start=True, stop=True)
                    last.then_inc(m_mm, 1)
                pe.wait_ge(m_red, 16 * (p + 1))
                nc.tensor.transpose(sc[2][0:2 * TB, 0:P], mx[:, :], ident).then_inc(m_tr, 1)
                pe.wait_ge(m_in, 48 * (p + 1))

            def enter_pair(i, k):
                p = 2 * i + k
                pe.wait_ge(qk_in[k], 16 * LOADS * (i + 1))
                with pe.If(fast == 0):
                    maxima(p, k)

            def untangle(p, k):
                pe.wait_ge(acc_ok, p + 1)
                for c in range(4):
                    last = nc.tensor.transpose(acc[k][:, c * P:(c + 1) * P], acc_s[:, c * P:(c + 1) * P], ident)
                last.then_inc(acc_tr, 1)

            def ranks():
                pe.wait_ge(pick_ok, 1)
                nc.tensor.matmul(acc[1][:, 0:T * E], before, cnt[:, 0, :, :], start=True, stop=True)
                nc.tensor.matmul(acc[1][:, T * E:2 * T * E], ones, cnt[:, 0, :, :], start=True,
                                 stop=True).then_inc(rank_mm, 1)
                pe.wait_ge(rank_ok, 1)

            def attend(i, first, last_iter):
                for s in range(2 * KB):
                    k, kb = s // KB, s % KB
                    p = 2 * i + k
                    if s + 1 < 2 * KB or not last_iter:
                        nk, nkb = ((s + 1) // KB) % 2, (s + 1) % KB
                        if nkb == 0:
                            enter_pair(i + (s + 1) // (2 * KB), nk)
                        for a in range(2):
                            u = 2 * (s + 1) + a
                            if s + 1 == 2 * KB:
                                pe.wait_ge(e_ok, 32 * i + 31 + a)
                                scores(nk, a, a, nkb)
                            else:
                                if u >= 3:
                                    pe.wait_ge(e_ok, 32 * i + u - 2)
                                scores(nk, u % 3, a, nkb)
                    if kb == 0:
                        if first and k == 1:
                            ranks()
                        pe.wait_ge(v_ok, p + 1)
                        if not (first and k == 0):
                            wait(pe, norm_ok, p - 1)
                    pe.wait_ge(e_ok, 32 * i + 2 * s + 2)
                    for a in range(2):
                        for half in range(2):
                            j = 2 * a + half
                            mm = nc.tensor.matmul(acc[k][32 * j:32 * j + 32, :], v_aug[k][:, kb, a, :],
                                                  probs[(2 * s + a) % 4][:, half, :],
                                                  start=(kb == 0), stop=(kb == KB - 1))
                    mm.then_inc(pv_mm, 1)
                    if kb == 1 and not (first and k == 0):
                        untangle(p - 1, 1 - k)

            enter_pair(0, 0)
            for a in range(2):
                scores(0, a, a, 0)
            attend(0, True, False)
            with pe.Fori(1, MID) as i:
                attend(i, False, False)

            def tile_in(i, j):
                pe.wait_ge(xt_in[j % 4], 16 * (BODY // 4 * i + j // 4 + 1))
                nc.tensor.transpose(sc[2][:, (j % 2) * CH:(j % 2) * CH + P], xt[j % 4], ident).then_inc(xt_tr, 1)

            def layer_one(t, j):
                pe.wait_ge(xsT_ok, t + 1)
                for c in range(FC):
                    mm = nc.tensor.matmul(sc[0][:, (j % 2) * CH + c * P:(j % 2) * CH + (c + 1) * P],
                                          w_tile[j % 4][:, c * P:(c + 1) * P], xsT[j % 2],
                                          start=True, stop=True)
                mm.then_inc(h_mm, 1)

            def layer_two(t, j):
                pe.wait_ge(relu_ok, t + 1)
                wait(pe, y_ok, t - 1)
                for c in range(FC):
                    mm = nc.tensor.matmul(sc[1][:, (j % 2) * CH:(j % 2) * CH + D], hT[j % 2][:, c, :],
                                          w_tile[j % 4][:, W2_AT + c * D:W2_AT + (c + 1) * D],
                                          start=(c == 0), stop=(c == FC - 1))
                mm.then_inc(y_mm, 1)

            def expert_body(i, first):
                for j in range(BODY):
                    t = BODY * i + j
                    tile_in(i, j + 1)
                    layer_one(t, j)
                    if not (first and j == 0):
                        layer_two(t - 1, j + BODY - 1)

            pe.wait_ge(e_ok, 32 * MID + 2)
            tile_in(0, 0)
            expert_body(0, True)
            with pe.Fori(1, SLOT_TILES // BODY) as i:
                expert_body(i, False)
            layer_two(SLOT_TILES - 1, BODY - 1)

            pe.wait_ge(y_ok, SLOT_TILES)
            pe.wait_ge(xsT_ok, SLOT_TILES + 1)
            with pe.Fori(MID, ITERS - 1) as i:
                attend(i, False, False)
            attend(ITERS - 1, False, True)
            untangle(PAIRS - 1, 1)

            def project(g):
                pe.wait_ge(oT_ok, g + 1)
                wait(pe, fin_ok, g - 1)
                for n in range(G):
                    mm = nc.tensor.matmul(sc[1][:, (g % 2) * CH + n * D:(g % 2) * CH + (n + 1) * D],
                                          oT[g % 2][:, n, :], woT[:, :], start=True, stop=True)
                mm.then_inc(o_mm, 1)

            pe.wait_ge(norm_ok, PAIRS)
            for g in range(T // G):
                wait(pe, oT_ok, g - 1)
                for n in range(G):
                    t = g * G + n
                    last = nc.tensor.transpose(sc[0][:, (g % 2) * CH + n * P:(g % 2) * CH + (n + 1) * P],
                                               att[:, t // TB, t % TB, :], ident)
                last.then_inc(o_tr, 1)
                if g > 0:
                    project(g - 1)
            project(T // G - 1)

        @block.scalar
        def _(act):
            act.dma_start(const[:, :], const_d).then_inc(const_in, 16)
            for k, w in enumerate((wq_d, wk_d, wv_d, wo_d)):
                act.dma_start(wr[:, k, :], w).then_inc(w_in, 16)
            act.dma_start(rows[0:32, :], b1_d.rearrange("e (c p) -> (e c) p", p=P)).then_inc(rows_in, 16)
            act.dma_start(rows[32:40, :], gamma_d).then_inc(rows_in, 16)
            act.dma_start(rows[40:48, :], beta_d).then_inc(rows_in, 16)
            act.dma_start(wvg[:, D:D + E], wg_d).then_inc(gate_in, 16)

            for k in range(2):
                act.wait_ge(ln_var, k + 1)
                nc.scalar.activation(small[:, 9 + k, :], small[:, 3 + 2 * k, :], ACT.Sqrt).then_inc(ln_sqrt, 1)

            def high(n):
                act.wait_ge(rope_sum, n + 1)
                wait(act, part_out[n % 3], 16 * PARTS * (n // 3))
                nc.scalar.copy(part[:, n % 3, 0, :], prod_c[n % 4]).then_inc(hi_ok, 1)

            def squares(n):
                wait(act, norm_mm, n - 1)
                nc.scalar.activation(square[n % 2][:, :], prod_c[n % 4], ACT.Square).then_inc(sq_ok, 1)

            def middle(n):
                act.wait_ge(mid_in, n + 1)
                nc.scalar.copy(part[:, n % 3, 1, :], prod_c[n % 4]).then_inc(mid_ok, 1)

            def columns(b):
                act.wait_ge(xtr, b + 1)
                nc.scalar.copy(xnT[:, b * S:(b + 1) * S], sc[2][:, :]).then_inc(xtr_out, 1)

            columns(0)
            for b in range(B):
                for c in range(2):
                    for g in range(2):
                        n = 4 * b + 2 * c + g
                        high(n)
                        squares(n)
                        q = n
                        act.wait_ge(v_mm, q + 1)
                        for u in range(2):
                            t = 2 * q + u
                            src = acc[0][:, u * (D + E):(u + 1) * (D + E)]
                            nc.scalar.copy(v_all[:, b * PB:(b + 1) * PB, t % TB, :],
                                           src[:, 0:D].rearrange("p (a w) -> p a w", a=PB)).then_inc(v_out, 2)
                            nc.scalar.copy(score[:, t, :], src[:, D:D + E]).then_inc(v_out, 2)
                        if c == 1 and g == 1 and b + 1 < B:
                            columns(b + 1)
                        middle(n)

            def attend(i):
                for u in range(4 * KB):
                    s = u // 2
                    act.wait_ge(s_mm, 32 * i + u + 1)
                    if u % 2 == 0:
                        wait(act, pv_mm, 16 * i + s - 1)
                    nc.scalar.activation(probs[u % 4], sc[u % 32 % 3][:, :].rearrange("p (h c) -> p h c", h=2),
                                         ACT.Exp, scale=SCALE).then_inc(e_ok, 1)
                    if u == 2 * KB - 1 and isinstance(i, int):
                        act.wait_ge(gap_ok, 1)
                        nc.scalar.activation(small[:, 1, :], small[:, 0, :], ACT.Exp).then_inc(gate_exp, 1)

            act.wait_ge(flag_ok, 1)
            attend(0)
            with act.Fori(1, MID) as i:
                attend(i)

            def exp_unit(i, u):
                act.wait_ge(s_mm, 32 * i + u + 1)
                if u % 2 == 0:
                    wait(act, pv_mm, 16 * i + u // 2 - 1)
                nc.scalar.activation(probs[u % 4], sc[u % 3][:, :].rearrange("p (h c) -> p h c", h=2),
                                     ACT.Exp, scale=SCALE).then_inc(e_ok, 1)

            exp_unit(MID, 0)
            exp_unit(MID, 1)

            def relu(i, j):
                t = BODY * i + j
                act.wait_ge(h_mm, t + 1)
                wait(act, y_mm, t - 1)
                for c in range(FC):
                    a = nc.scalar.activation(hT[j % 2][:, c, :], sc[0][:, (j % 2) * CH + c * P:
                                                                       (j % 2) * CH + (c + 1) * P],
                                             ACT.Relu, bias=w_tile[j % 4][:, B1_AT + c:B1_AT + c + 1])
                a.then_inc(relu_ok, 1)

            for j in range(BODY):
                relu(0, j)
            with act.Fori(1, SLOT_TILES // BODY) as i:
                for j in range(BODY):
                    relu(i, j)

            for u in range(2, 4 * KB):
                exp_unit(MID, u)
            with act.Fori(MID + 1, ITERS) as i:
                attend(i)

            for g in range(T // G):
                act.wait_ge(o_tr, g + 1)
                wait(act, o_mm, g - 1)
                nc.scalar.copy(oT[g % 2], sc[0][:, (g % 2) * CH:(g % 2 + 1) * CH].rearrange("p (t c) -> p t c", t=G)
                               ).then_inc(oT_ok, 1)

        @block.vector
        def _(v):
            chain = [0]

            def link(ins):
                chain[0] += 1
                ins.then_inc(dve, 1)
                v.wait_ge(dve, chain[0])

            nc.vector.memset(ones, 1.0)
            for k in range(2):
                nc.vector.memset(qs[k][64:96, :, :], 0.0)
                last = nc.vector.memset(ks[k][64:96, :, :], 1.0)
            last.then_inc(stack_ok, 1)

            for b in range(B):
                v.wait_ge(x_in[b], 16)
                for t in range(b * TB, (b + 1) * TB):
                    last = nc.vector.bn_stats(stats[:, t, :], x[:, t, :])
            link(last)
            for t in range(T):
                last = nc.vector.bn_aggr(mv[:, t, :], stats[:, t, :])
            link(last)
            mean, var = mv[:, :, 0], mv[:, :, 1]

            def inverse_root(k, dst):
                val, rec_ = small[:, 2 + 2 * k, :], small[:, 3 + 2 * k, :]
                nc.vector.reciprocal(rec_, val).then_inc(ln_var, 1)
                y0, tmp, y = small[:, 9 + k, :], small[:, 11, :], small[:, dst, :]
                v.wait_ge(ln_sqrt, k + 1)
                link(nc.vector.tensor_tensor(tmp, y0, y0, ALU.mult))
                link(nc.vector.tensor_tensor(tmp, tmp, val, ALU.mult))
                link(nc.vector.tensor_scalar(tmp, tmp, -0.5, 1.5, ALU.mult, ALU.add))
                link(nc.vector.tensor_tensor(y, y0, tmp, ALU.mult))

            link(nc.vector.tensor_scalar(small[:, 2, :], var, 1e-5, None, ALU.add))
            inverse_root(0, 6)
            rstd = small[:, 6, :]
            link(nc.vector.tensor_tensor(small[:, 4, :], var, rstd, ALU.mult))
            link(nc.vector.tensor_tensor(small[:, 4, :], small[:, 4, :], rstd, ALU.mult))
            link(nc.vector.tensor_scalar(small[:, 4, :], small[:, 4, :], 1e-6, None, ALU.add))
            inverse_root(1, 7)
            link(nc.vector.tensor_tensor(small[:, 8, :], mean, rstd, ALU.mult))
            for t in range(T):
                nc.vector.tensor_scalar(xn[:, t, :], x[:, t, :], small[:, 6, t:t + 1], small[:, 8, t:t + 1],
                                        ALU.mult, ALU.subtract).then_inc(xn_ok, 1)

            v.wait_ge(wtr, 1)
            ps = sc[0][:, 0:4 * D].rearrange("p (k d) -> p k d", k=4)
            for s in range(2):
                nc.vector.tensor_copy(wT[:, 2 * s, :], ps[:, s, :]).then_inc(wtr_out, 1)
                two = ps[:, s, :].rearrange("p (i r) -> p i r", r=2)
                rot = wT[:, 2 * s + 1, :].rearrange("p (i r) -> p i r", r=2)
                nc.vector.tensor_scalar(rot[:, :, 0], two[:, :, 1], -1.0, None, ALU.mult)
                nc.vector.tensor_copy(rot[:, :, 1], two[:, :, 0]).then_inc(wtr_out, 1)
            nc.vector.tensor_copy(wvg[:, 0:D], ps[:, 2, :]).then_inc(wtr_out, 1)
            nc.vector.tensor_copy(woT[:, :], ps[:, 3, :]).then_inc(wtr_out, 1)
            v.wait_ge(rtr, 1)
            nc.vector.tensor_copy(w_all[:, :, B1_AT:B1_AT + FC],
                                  sc[0][:, CH:CH + 32].rearrange("p (e c) -> p e c", e=E)).then_inc(rtr_out, 1)
            nc.vector.tensor_copy(w_all[:, :, GA_AT], sc[0][:, CH + 32:CH + 40]).then_inc(rtr_out, 1)
            nc.vector.tensor_copy(w_all[:, :, BE_AT], sc[0][:, CH + 40:CH + 48]).then_inc(rtr_out, 1)

            v.wait_ge(rope_in, 32)
            nc.vector.tensor_copy(head_of[:, :], head_row).then_inc(head_ok, 1)

            def rotate(n, c, s):
                v.wait_ge(proj, n + 1)
                wait(v, lo_ok, n - 3)
                pos = slice(c * CH, (c + 1) * CH)
                nc.vector.tensor_tensor(prod_c[n % 4], sc[s][:, 0:CH], cos[:, pos], ALU.mult).then_inc(rope_out, 1)
                nc.vector.tensor_tensor(prod_s[n % 4], sc[s][:, CH:2 * CH], sin[:, pos], ALU.mult
                                        ).then_inc(rope_out, 1)

            def rest_one(n, b, c, s):
                v.wait_ge(rope_sum, n + 1)
                v.wait_ge(hi_ok, n + 1)
                v.wait_ge(sq_ok, n + 1)
                nc.vector.tensor_tensor(prod_c[n % 4], prod_c[n % 4], part[:, n % 3, 0, :], ALU.subtract
                                        ).then_inc(mid_in, 1)

            def rest_two(n):
                v.wait_ge(mid_ok, n + 1)
                nc.vector.tensor_tensor(part[:, n % 3, 2, :], prod_c[n % 4], part[:, n % 3, 1, :], ALU.subtract
                                        ).then_inc(lo_ok, 1)

            order = steps()
            def batch_norms(b):
                v.wait_ge(norm_mm, 4 * (b + 1))
                nc.vector.reduce_max(norms[:, b:b + 1], acc[1][:, :], AX.X).then_inc(norm_in, 1)

            for n, b, c, s in order:
                if n % 4 == 1 and b > 0:
                    batch_norms(b - 1)
                rotate(n, c, s)
                if n >= 1:
                    rest_one(*order[n - 1])
                if n >= 2:
                    rest_two(n - 2)
            rest_one(*order[-1])
            rest_two(len(order) - 2)
            rest_two(len(order) - 1)
            batch_norms(B - 1)

            v.wait_ge(bound_tr, 1)
            rows4 = acc[1][0:B, 0:P].rearrange("b (s c h) -> b s c h", s=2, c=2)
            for k in range(2):
                link(nc.vector.reduce_max(norm_b[:, k, :], rows4[:, k, :, 0:H].rearrange("b c h -> b h c"), AX.X))
            link(nc.vector.tensor_tensor(norm_b[:, 2, :], norm_b[:, 0, :], norm_b[:, 1, :], ALU.mult))
            nc.vector.reduce_max(norm_m[:, :], norm_b[:, 2, :], AX.X).then_inc(bound_ok, 1)
            v.wait_ge(bound_tr2, 1)
            link(nc.vector.reduce_max(flag_f[:, 0, :], acc[1][0:1, P:P + B], AX.X))
            link(nc.vector.tensor_scalar(flag_f[:, 1, :], flag_f[:, 0, :], (SAFE / SCALE) ** 2, None, ALU.is_le))
            nc.vector.tensor_copy(flag[:, :], flag_f[:, 1, :]).then_inc(flag_ok, 1)

            v.wait_ge(flag_ok, 1)
            fast = v.value_load(flag[0:1, 0:1], min_val=0, max_val=1)

            def maxima(p):
                for n in range(2 * TB):
                    v.wait_ge(m_mm, 16 * p + n + 1)
                    nc.vector.reduce_max(mx[:, n:n + 1], sc[n % 2][:, :], AX.X).then_inc(m_red, 1)
                v.wait_ge(m_tr, p + 1)
                wait(v, m_in, 48 * p)
                base = 5 * p
                nc.vector.tensor_scalar(mrow[:, 0, :], sc[2][0:2 * TB, 0:P], -1.0, None, ALU.mult).then_inc(m_chain, 1)
                v.wait_ge(m_chain, base + 1)
                nc.vector.tensor_copy(mpart[:, 0, :], mrow[:, 0, :]).then_inc(m_chain, 1)
                v.wait_ge(m_chain, base + 2)
                nc.vector.tensor_tensor(mrow[:, 1, :], mrow[:, 0, :], mpart[:, 0, :], ALU.subtract
                                        ).then_inc(m_chain, 1)
                v.wait_ge(m_chain, base + 3)
                nc.vector.tensor_copy(mpart[:, 1, :], mrow[:, 1, :]).then_inc(m_chain, 1)
                v.wait_ge(m_chain, base + 4)
                nc.vector.tensor_tensor(mrow[:, 2, :], mrow[:, 1, :], mpart[:, 1, :], ALU.subtract
                                        ).then_inc(m_chain, 1)
                v.wait_ge(m_chain, base + 5)
                nc.vector.tensor_copy(mpart[:, 2, :], mrow[:, 2, :]).then_inc(m_split, 1)

            def normalise(p, k):
                v.wait_ge(acc_tr, p + 1)
                ps = acc[k][:, :].rearrange("p (c a h w) -> p c a h w", c=4, a=2, h=2)
                for a in range(2):
                    nc.vector.reciprocal(rec[:, 2 * a:2 * a + 2, :], ps[:, :, a, :, DK].rearrange("p c h -> p h c")
                                         ).then_inc(rec_ok, 1)
                v.wait_ge(rec_ok, 2 * (p + 1))
                for a in range(2):
                    for h in range(2):
                        dst = att[:, bass.ds(p // PB, 1), 4 * h:4 * h + 4,
                                  bass.ds((p % PB) * 2 * DK + a * DK, DK)]
                        m = nc.vector.tensor_tensor(dst.rearrange("p o c d -> p (o c) d"), ps[:, :, a, h, 0:DK],
                                                    rec[:, 2 * a + h, :].unsqueeze(2).to_broadcast([P, 4, DK]),
                                                    ALU.mult)
                m.then_inc(norm_ok, 1)

            def take(p, k):
                v.wait_ge(pv_mm, 8 * (p + 1))
                nc.vector.tensor_copy(acc_s[:, :], acc[k][:, :]).then_inc(acc_ok, 1)

            def route():
                for t in range(T):
                    last = nc.vector.max(top[:, t, :], score[:, t, :])
                link(last)
                for t in range(T):
                    last = nc.vector.max_index(topi[:, t, :], top[:, t, :], score[:, t, :])
                link(last)
                nc.vector.tensor_tensor(small[:, 0, :], top[:, :, 1], top[:, :, 0], ALU.subtract).then_inc(gap_ok, 1)
                link(nc.vector.tensor_copy(topf[:, :, :], topi[:, :, 0:2]))
                for k in range(2):
                    link(nc.vector.tensor_tensor(pick[:, k, :, :], iota_e.unsqueeze(1).to_broadcast([P, T, E]),
                                                 topf[:, :, k:k + 1].to_broadcast([P, T, E]), ALU.is_equal))
                nc.vector.tensor_tensor(cnt[:, 0, :, :], pick[:, 0, :, :], pick[:, 1, :, :], ALU.add
                                        ).then_inc(pick_ok, 1)

            def take_ranks():
                v.wait_ge(rank_mm, 1)
                nc.vector.tensor_copy(rank[:, :, :, :], acc[1][:, :].rearrange("p (a t e) -> p a t e", a=2, e=E)
                                      ).then_inc(rank_ok, 1)

            def place():
                v.wait_ge(gate_exp, 1)
                e, w1, w2, ws = small[:, 1, :], small[:, 2, :], small[:, 3, :], small[:, 4, :]
                link(nc.vector.tensor_scalar(w2, e, 1.0, None, ALU.add))
                link(nc.vector.reciprocal(w1, w2))
                link(nc.vector.tensor_tensor(w2, e, w1, ALU.mult))
                link(nc.vector.tensor_tensor(ws, w1, w2, ALU.add))

                v.wait_ge(rank_ok, 1)
                link(nc.vector.tensor_copy(cnt[:, 1, :, :], rank[:, 1, :, :]))
                a, shift = 1, 1
                while shift < T:
                    nxt = 3 - a
                    nc.vector.tensor_copy(cnt[:, nxt, 0:shift, :], cnt[:, a, 0:shift, :])
                    link(nc.vector.tensor_tensor(cnt[:, nxt, shift:T, :], cnt[:, a, shift:T, :],
                                                 cnt[:, a, 0:T - shift, :], ALU.add))
                    a, shift = nxt, 2 * shift
                incl = cnt[:, a, :, :]
                total = incl[:, T - 1, :]
                link(nc.vector.tensor_scalar(exp_s[:, 0, :], total, float(P - 1), None, ALU.add))
                link(nc.vector.tensor_copy(exp_i[:, 0, :], exp_s[:, 0, :]))
                link(nc.vector.tensor_scalar(exp_i[:, 1, :], exp_i[:, 0, :], 7, None, ALU.arith_shift_right))
                link(nc.vector.tensor_copy(exp_s[:, 0, :], exp_i[:, 1, :]))
                link(nc.vector.tensor_copy(exp_s[:, 1, :], exp_s[:, 0, :]))
                a2, shift = 1, 1
                while shift < E:
                    nxt = 3 - a2
                    nc.vector.tensor_copy(exp_s[:, nxt, 0:shift], exp_s[:, a2, 0:shift])
                    link(nc.vector.tensor_tensor(exp_s[:, nxt, shift:E], exp_s[:, a2, shift:E],
                                                 exp_s[:, a2, 0:E - shift], ALU.add))
                    a2, shift = nxt, 2 * shift
                ends = exp_s[:, a2, :]
                link(nc.vector.tensor_tensor(exp_s[:, 3, :], ends, exp_s[:, 0, :], ALU.subtract))
                link(nc.vector.tensor_scalar(exp_s[:, 3, :], exp_s[:, 3, :], float(P), None, ALU.mult))
                pos = cnt[:, 3, :, :]
                link(nc.vector.tensor_tensor(pos, incl, rank[:, 1, :, :],
                                             ALU.subtract))
                link(nc.vector.tensor_tensor(pos, pos, rank[:, 0, :, :], ALU.add))
                link(nc.vector.tensor_tensor(pos, pos, exp_s[:, 3:4, :].to_broadcast([P, T, E]), ALU.add))
                for k in range(2):
                    link(nc.vector.tensor_tensor(cnt[:, 0, :, :], pos, pick[:, k, :, :], ALU.mult))
                    link(nc.vector.reduce_sum(slot_f[:, k, :], cnt[:, 0, :, :], AX.X))
                    nc.vector.tensor_copy(slot[:, k, :], slot_f[:, k, :]).then_inc(slot_ok, 1)
                own_cmp = cnt[0:1, :, :, :].rearrange("p a t e -> p (a t) e")[:, 0:SLOT_TILES + 2, :]
                link(nc.vector.tensor_tensor(own_cmp,
                                             iota_t[0:1, :].unsqueeze(2).to_broadcast([1, SLOT_TILES + 2, E]),
                                             exp_s[0:1, a2:a2 + 1, :].to_broadcast([1, SLOT_TILES + 2, E]), ALU.is_ge))
                link(nc.vector.reduce_sum(owner_f[:, 0, :], own_cmp, AX.X))
                link(nc.vector.tensor_scalar(owner_f[:, 1, :], owner_f[:, 0, :], float(E - 1), None, ALU.min))
                nc.vector.tensor_copy(owner[:, :], owner_f[:, 1, :]).then_inc(owner_ok, 1)


            def residuals():
                v.wait_ge(xh_ok, T)
                for t in range(T):
                    nc.vector.scalar_tensor_tensor(out=x[:, t, :], in0=xn[:, t, :], scalar=small[:, 4, t:t + 1],
                                                   in1=x[:, t, :], op0=ALU.mult, op1=ALU.add).then_inc(base_ok, 1)

            def copy_v(p, k):
                wait(v, pv_mm, 8 * (p - 1))
                nc.vector.tensor_copy(v_aug[k][:, :, :, 0:DK],
                                      v_all[:, bass.ds(p, 1), :, :].rearrange("p o k (a d) -> p (o k) a d", a=2)
                                      ).then_inc(v_ok, 1)

            def attend(i, last_iter, before_take, after_take):
                for k in range(2):
                    p = 2 * i + k
                    if not isinstance(p, int) or p > 0:
                        normalise(p - 1, 1 - k)
                    if not (last_iter and k == 1):
                        copy_v(p + 1, 1 - k)
                    if before_take[k]:
                        before_take[k]()
                    if not (last_iter and k == 1):
                        with v.If(fast == 0):
                            maxima(p + 1)
                    take(p, k)
                    if after_take[k]:
                        after_take[k]()

            with v.If(fast == 0):
                maxima(0)
            nothing = (None, None)
            v.wait_ge(v_one, 2)
            v.wait_ge(v_out, 4 * T)
            copy_v(0, 0)
            attend(0, False, (route, None), (take_ranks, place))
            attend(1, False, nothing, (residuals, None))
            with v.Fori(2, MID) as i:
                attend(i, False, nothing, nothing)

            v.wait_ge(exp_in, 16 * 3 * E)

            def weights(t, j):
                e = v.value_load(owner[0:1, bass.ds(t, 1)], min_val=0, max_val=E - 1)
                wait(v, y_ok, t - 3)
                nc.vector.tensor_copy(w_tile[j % 4],
                                      w_all[:, bass.ds(e, 1), :].rearrange("p o w -> p (o w)")).then_inc(w_ok, 1)

            def columns(t, j):
                v.wait_ge(xt_tr, t + 1)
                v.wait_ge(w_ok, t + 1)
                nc.vector.tensor_scalar(xsT[j % 2], sc[2][:, (j % 2) * CH:(j % 2) * CH + P],
                                        w_tile[j % 4][:, GA_AT:GA_AT + 1], w_tile[j % 4][:, BE_AT:BE_AT + 1],
                                        ALU.mult, ALU.add).then_inc(xsT_ok, 1)

            def rows_out(i, j):
                t = BODY * i + j
                v.wait_ge(y_mm, t + 1)
                wait(v, y_out[j % 2], 16 * (BODY // 2 * i + j // 2))
                nc.vector.tensor_tensor(ys[j % 2], sc[1][:, (j % 2) * CH:(j % 2) * CH + D],
                                        w_tile[j % 4][:, B2_AT:B2_AT + D], ALU.add).then_inc(y_ok, 1)

            def expert_body(i, first):
                for j in range(BODY):
                    t = BODY * i + j
                    columns(t + 1, j + 1)
                    if not (first and j < 2):
                        rows_out(i, j - 2)
                    weights(t + 2, j + 2)

            weights(0, 0)
            weights(1, 1)
            columns(0, 0)
            expert_body(0, True)
            with v.Fori(1, SLOT_TILES // BODY) as i:
                expert_body(i, False)
            rows_out(SLOT_TILES // BODY - 1, BODY - 2)
            rows_out(SLOT_TILES // BODY - 1, BODY - 1)

            def merge(group):
                def add():
                    v.wait_ge(gathered, 16 * 2 * T)
                    for src, wk in ((xn, 2), (xh, 3)):
                        for t in range(group * 4, group * 4 + 4):
                            last = nc.vector.scalar_tensor_tensor(out=x[:, t, :], in0=src[:, t, :],
                                                                  scalar=small[:, wk, t:t + 1], in1=x[:, t, :],
                                                                  op0=ALU.mult, op1=ALU.add)
                        link(last)
                return add

            with v.Fori(MID, MERGE[0]) as i:
                attend(i, False, nothing, nothing)
            for i in range(*MERGE):
                n = 2 * (i - MERGE[0])
                attend(i, False, nothing, (merge(n), merge(n + 1)))
            attend(ITERS - 1, True, nothing, nothing)
            normalise(PAIRS - 1, 1)

            for g in range(T // G):
                v.wait_ge(o_mm, g + 1)
                wait(v, fin_out[g % 2], 16 * (g // 2))
                nc.vector.tensor_tensor(fin[g % 2],
                                        sc[1][:, (g % 2) * CH:(g % 2 + 1) * CH].rearrange("p (t d) -> p t d", t=G),
                                        x[:, g * G:(g + 1) * G, :], ALU.add).then_inc(fin_ok, 1)


def rope_tables():
    inv_freq = (np.float32(1.0) / np.power(np.float32(10000.0), np.arange(0, DK, 2, dtype=np.float32)
                                           / np.float32(DK))).astype(np.float32)
    angle = np.arange(S, dtype=np.float32)[None, :] * np.tile(np.repeat(inv_freq, 2), H)[:, None]
    return np.cos(angle).astype(np.float32), np.sin(angle).astype(np.float32)


def constants():
    c = np.zeros((P, 4 * P), np.float32)
    i = np.arange(P)
    c[:, 0:P] = np.eye(P)
    c[:, P:2 * P] = i[:, None] < i[None, :]
    c[:, 2 * P:2 * P + H] = (i[:, None] // DK) == np.arange(H)[None, :]
    c[:, 3 * P:3 * P + E] = np.arange(E)
    c[:, 3 * P + E:3 * P + E + SLOT_TILES + 2] = np.arange(SLOT_TILES + 2)
    return c


INPUTS = ["L0_attn_x", "L0_attn_W_q", "L0_attn_W_k", "L0_attn_W_v", "L0_attn_W_o", "L0_ffn_Wg", "L0_ffn_gamma",
          "L0_ffn_beta", "L0_ffn_W1", "L0_ffn_b1", "L0_ffn_W2", "L0_ffn_b2"]


def kernel(**inputs):
    import concourse.bacc as bacc
    from concourse.bass_utils import run_bass_kernel_spmd

    nc = bacc.Bacc("TRN2", target_bir_lowering=False, num_devices=1)
    arrays, args = {}, []
    cos, sin = rope_tables()
    given = [(n, np.ascontiguousarray(inputs[n])) for n in INPUTS]
    given += [("rope_cos", cos), ("rope_sin", sin), ("shape_constants", constants())]
    for name, a in given:
        arrays[name] = a
        args.append(nc.dram_tensor(name, a.shape, mybir.dt.from_np(a.dtype), kind="ExternalInput").ap())
    args.append(nc.dram_tensor("out", (B, S, D), F32, kind="ExternalOutput").ap())
    build(nc, *args)
    return run_bass_kernel_spmd(nc, [arrays], core_ids=[0]).results[0]["out"]
```

```python
import math
from contextlib import ExitStack

import numpy as np
import concourse.bass as bass
from concourse import mybir

F32 = mybir.dt.float32
BF16 = mybir.dt.bfloat16
I32 = mybir.dt.int32
U32 = mybir.dt.uint32
ALU = mybir.AluOpType
ACT = mybir.ActivationFunctionType
AX = mybir.AxisListType

P = 128
B, S, D = 4, 1024, 128
H, DK = 16, 8
E, F = 8, 512
T = B * S // P
TB = S // P
CH = 512
PAIRS = B * H // 2
PB = PAIRS // B
PARTS = 3
ROWS = PARTS * PARTS * DK
KR = ROWS + PARTS
LOADS = 2 * PARTS * PARTS
PR = 4
SECOND = 8
LATE = 2
STEPS = 4 * B
HALF = CH // P
KB = S // P
FC = F // P
SLOT_TILES = 72
BODY = 8
XS_TILES = SLOT_TILES + 4
W_LEN = F + F + FC + 2 + D
W2_AT, B1_AT, GA_AT, BE_AT, B2_AT = F, 2 * F, 2 * F + FC, 2 * F + FC + 1, 2 * F + FC + 2
SCALE = 1.0 / math.sqrt(DK)
SAFE = 60.0
MID = 4
ITERS = PAIRS // 2
MERGE = (11, 15)
G = 4
LAST_GROUPS = (B - 1) * TB // G


def build(nc, x_d, wq_d, wk_d, wv_d, wo_d, wg_d, gamma_d, beta_d, w1_d, b1_d, w2_d, b2_d, cos_d, sin_d, const_d,
          out_d):
    ctx = ExitStack()
    with ctx:
        def sb(name, shape, dt=F32):
            return ctx.enter_context(nc.sbuf_tensor(name, shape, dt))

        def sem(name):
            return ctx.enter_context(nc.semaphore(name))

        parts_d = [nc.dram_tensor(f"parts_{s}", [PARTS, PAIRS, 2 * DK, S], BF16, kind="Internal").ap()
                   for s in "qk"]
        xs_d = nc.dram_tensor("slot_in", [XS_TILES * P, D], F32, kind="Internal").ap()
        ys_d = nc.dram_tensor("slot_out", [SLOT_TILES * P, D], F32, kind="Internal").ap()

        x = sb("x", [P, T, D])
        xn = sb("xn", [P, T, D])
        xh = sb("xh", [P, T, D])
        xnT = sb("xnT", [P, T * P])
        att = xnT[:, :].rearrange("p (b q w) -> p b q w", b=B, q=TB)
        v_all = sb("v_all", [P, PAIRS, KB, 2 * DK])
        ring = sb("ring", [P, 8, CH])
        prod_c = [ring[:, k, :] for k in range(4)]
        prod_s = [ring[:, 4 + k, :] for k in range(4)]
        probs = [ring[:, 2 * k:2 * k + 2, :] for k in range(4)]
        work = sb("work", [P, PR * PARTS * CH // 2])
        part = work[:, :].bitcast(BF16).rearrange("p (k i c) -> p k i c", k=PR, i=PARTS)
        tables = sb("tables", [P, 3 * W_LEN])
        cos, sin = tables[:, 0:S], tables[:, S:2 * S]
        const = sb("const", [P, 4 * P])
        ident, before = const[:, 0:P], const[:, P:2 * P]
        head_row = const[:, 2 * P:2 * P + 32]
        iota_e, iota_t = const[:, 3 * P:3 * P + E], const[:, 3 * P + E:3 * P + E + SLOT_TILES + 2]
        early = sb("early", [P, 10 * D])
        wr = early[:, 0:4 * D].rearrange("p (k d) -> p k d", k=4)
        wT = early[:, 4 * D:8 * D].rearrange("p (k d) -> p k d", k=4)
        ones, rows = early[:, 8 * D:9 * D], early[:, 9 * D:10 * D]
        wvg = sb("wvg", [P, D + E])
        woT = sb("woT", [P, D])
        w_all = sb("w_all", [P, E, W_LEN])
        w_tile = [tables[:, k * W_LEN:(k + 1) * W_LEN] for k in range(3)] + [early[:, 0:W_LEN]]
        qs = [sb(f"qs{k}", [P, 2, S], BF16) for k in range(2)]
        ks = [sb(f"ks{k}", [P, 2, S], BF16) for k in range(2)]
        v_aug = [sb(f"v_aug{k}", [P, KB, 2, 32]) for k in range(2)]
        rank_words = early[:, 0:4 * D]
        acc_s = sb("acc_s", [P, CH])
        rec = sb("rec", [P, 4, 4])
        stats = sb("stats", [P, T, 6])
        mv = sb("mv", [P, T, 2])
        small = sb("small", [P, 12, T])
        score = sb("score", [P, T, E])
        top = sb("top", [P, T, 8])
        topi = sb("topi", [P, T, 8], U32)
        topf = sb("topf", [P, T, 2])
        pick = sb("pick", [P, 2, T, E])
        cnt = sb("cnt", [P, 4, T, E])
        rank = rank_words[:, :].rearrange("p (a t e) -> p a t e", a=2, e=E)
        exp_s = sb("exp_s", [P, 4, E])
        exp_i = sb("exp_i", [P, 2, E], I32)
        slot_f = sb("slot_f", [P, 2, T])
        slot = sb("slot", [P, 2, T], U32)
        owner_f = sb("owner_f", [1, 2, SLOT_TILES + 2])
        owner = sb("owner", [1, SLOT_TILES + 2], I32)
        head_of = sb("head_of", [P, 32], BF16)
        square = [sb(f"square{k}", [P, CH], BF16) for k in range(2)]
        norms = sb("norms", [P, B])
        norm_b = sb("norm_b", [B, 3, H])
        norm_m = sb("norm_m", [B, 1])
        flag_f = sb("flag_f", [1, 1, 1])
        flag = sb("flag", [1, 1], I32)
        xt, ys = ([work[:, (k + 2 * n) * P:(k + 2 * n + 2) * P].rearrange("p (u d) -> p u d", u=2)
                   for n in range(2)] for k in (0, 4))
        xsT = [work[:, k * P:(k + 1) * P] for k in (8, 9)]
        hT = [work[:, (10 + FC * k) * P:(10 + FC * (k + 1)) * P].rearrange("p (c n) -> p c n", c=FC) for k in range(2)]
        oT, fin = ([work[:, (k + n) * G * P:(k + n + 1) * G * P].rearrange("p (t c) -> p t c", t=G)
                    for n in range(2)] for k in (0, 2))
        mx = sb("mx", [P, 2 * TB])
        mrow = sb("mrow", [2 * TB, 3, P])
        mpart = sb("mpart", [2 * TB, PARTS, P], BF16)

        sc = [ctx.enter_context(nc.psum_tensor(f"sc{k}", [P, 2 * CH], F32)) for k in range(3)]
        acc = [ctx.enter_context(nc.psum_tensor(f"acc{k}", [P, CH], F32)) for k in range(2)]

        x_in = [sem(f"x_in{b}") for b in range(B)]
        w_in, rows_in, const_in, rope_in, gate_in, exp_in = (
            sem(n) for n in ("w_in", "rows_in", "const_in", "rope_in", "gate_in", "exp_in"))
        zeroed, scattered, gathered = sem("zeroed"), sem("scattered"), sem("gathered")
        stack_ok, slots_zero, v_zero, v_one, dve = (
            sem(n) for n in ("stack_ok", "slots_zero", "v_zero", "v_one", "dve"))
        ln_var, ln_sqrt, xn_ok, xh_ok = (sem(n) for n in ("ln_var", "ln_sqrt", "xn_ok", "xh_ok"))
        ln_ok, xh_scale, table_in = sem("ln_ok"), sem("xh_scale"), sem("table_in")
        ln_tiles = (slice(0, TB), slice(TB, T), slice(0, T))
        wtr, wtr_out, rtr, rtr_out = sem("wtr"), sem("wtr_out"), sem("rtr"), sem("rtr_out")
        xtr, xtr_out, proj, rope_out, v_mm, v_out = (sem(n) for n in
                                                     ("xtr", "xtr_out", "proj", "rope_out", "v_mm", "v_out"))
        rope_sum, hi_ok, mid_in, mid_ok, lo_ok = (sem(n) for n in
                                                            ("rope_sum", "hi_ok", "mid_in", "mid_ok", "lo_ok"))
        part_out = [sem(f"part_out{k}") for k in range(PR)]
        gap_ok, gate_exp, pick_ok, rank_mm, rank_ok, slot_ok, owner_ok = (sem(n) for n in
                                                                 ("gap_ok", "gate_exp", "pick_ok", "rank_mm", "rank_ok",
                                                                  "slot_ok", "owner_ok"))
        sq_ok, norm_mm, norm_in, bound_tr, bound_ok, bound_tr2, flag_ok, head_ok = (
            sem(n) for n in ("sq_ok", "norm_mm", "norm_in", "bound_tr", "bound_ok", "bound_tr2", "flag_ok",
                             "head_ok"))
        base_ok = sem("base_ok")
        qk_in = [sem(f"qk_in{k}") for k in range(2)]
        v_ok, s_mm, e_ok, pv_mm, acc_ok, acc_tr, norm_ok = (sem(n) for n in
                                                                   ("v_ok", "s_mm", "e_ok", "pv_mm",
                                                                    "acc_ok", "acc_tr", "norm_ok"))
        m_mm, m_red, m_tr, m_split, m_in, m_chain, rec_ok = (sem(n) for n in
                                                           ("m_mm", "m_red", "m_tr", "m_split", "m_in", "m_chain",
                                                            "rec_ok"))
        xt_tr, xsT_ok, w_ok, h_mm, relu_ok, y_mm, y_ok = (sem(n) for n in
                                                                        ("xt_tr", "xsT_ok", "w_ok", "h_mm",
                                                                         "relu_ok", "y_mm", "y_ok"))
        xt_in = [sem(f"xt_in{k}") for k in range(2)]
        y_out = [sem(f"y_out{k}") for k in range(2)]
        fin_out = [sem(f"fin_out{k}") for k in range(2)]
        o_tr, oT_ok, o_mm, fin_ok = (sem(n) for n in ("o_tr", "oT_ok", "o_mm", "fin_ok"))

        block = ctx.enter_context(nc.Block())

        def wait(eng, s, value):
            if not isinstance(value, int) or value > 0:
                eng.wait_ge(s, value)

        def steps():
            return [(4 * b + 2 * c + s, b, c, s) for b in range(B) for c in range(2) for s in range(2)]

        @block.sync
        def _(sp):
            for b in range(B):
                sp.dma_start(x[:, b * TB:(b + 1) * TB, :],
                             x_d[b].rearrange("(t p) d -> p t d", p=P)).then_inc(x_in[b], 16)
                if b == 0:
                    sp.dma_start(wr[:, 2, :], wv_d).then_inc(w_in, 16)
                    sp.dma_start(wr[:, 3, :], wo_d).then_inc(w_in, 16)
                    sp.dma_start(wvg[:, D:D + E], wg_d).then_inc(gate_in, 16)
            sp.dma_start(cos, cos_d).then_inc(rope_in, 16)
            sp.dma_start(sin, sin_d).then_inc(rope_in, 16)
            sp.dma_start(rows[0:32, :], b1_d.rearrange("e (c p) -> (e c) p", p=P)).then_inc(rows_in, 16)
            sp.dma_start(rows[32:40, :], gamma_d).then_inc(rows_in, 16)
            sp.dma_start(rows[40:48, :], beta_d).then_inc(rows_in, 16)
            def load_rows(p, k, side, i, j):
                r = (PARTS * i + j) * DK
                src = parts_d[side][(i, j)[side], bass.ds(p, 1), :, :].rearrange("o (a d) t -> (o d) a t", a=2)
                sp.dma_start((qs, ks)[side][k][r:r + DK, :, :], src).then_inc(qk_in[k], 16)

            stack = [(side, i, j) for side in range(2) for i in range(PARTS) for j in range(PARTS)]

            def load_pair(p, k):
                wait(sp, s_mm, 16 * (p - 1))
                for side, i, j in stack:
                    load_rows(p, k, side, i, j)

            first_pairs = [(k, k) + rows_ for k in range(2) for rows_ in stack]
            early_step = 2 * PR
            share = 3
            for n, b, c, s in steps():
                if n == early_step:
                    sp.wait_ge(stack_ok, 4)
                if n >= early_step:
                    for row_group in first_pairs[share * (n - early_step):share * (n - early_step + 1)]:
                        load_rows(*row_group)
                sp.wait_ge(lo_ok, n + 1)
                if PR <= n < early_step:
                    sp.wait_ge(part_out[n % PR], 16 * PARTS)
                for i in range(PARTS):
                    dst = parts_d[s][i, b * PB:(b + 1) * PB, :, c * CH:(c + 1) * CH]
                    sp.dma_start(dst.rearrange("a r t -> (a r) t"), part[:, n % PR, i, :]
                                 ).then_inc(part_out[n % PR], 16)
            for row_group in first_pairs[share * (STEPS - early_step):]:
                load_rows(*row_group)
            for e in range(E):
                sp.dma_start(w_all[:, e, 0:F], w1_d[e]).then_inc(exp_in, 16)
                sp.dma_start(w_all[:, e, W2_AT:W2_AT + F].rearrange("p (c d) -> p c d", c=FC),
                             w2_d[e].rearrange("(c p) d -> p c d", p=P)).then_inc(exp_in, 16)
                sp.dma_start(w_all[:, e, B2_AT:B2_AT + D], b2_d[e:e + 1, :].to_broadcast([P, D])).then_inc(exp_in, 16)
            for k in range(PR):
                sp.wait_ge(part_out[k], 16 * PARTS * (STEPS // PR))
            sp.wait_ge(flag_ok, 1)
            fast = sp.value_load(flag[0:1, 0:1], min_val=0, max_val=1)

            def store_max(p, k):
                with sp.If(fast == 0):
                    sp.wait_ge(m_split, p + 1)
                    for i in range(PARTS):
                        sp.dma_start(qs[k][ROWS + i:ROWS + i + 1, :, :].rearrange("o a (q c) -> o (a q) c", c=P),
                                     mpart[:, i, :]).then_inc(m_in, 16)

            def feed(i):
                load_pair(2 * i, 0)
                store_max(2 * i - 1, 1)
                load_pair(2 * i + 1, 1)
                store_max(2 * i, 0)

            store_max(0, 0)
            with sp.Fori(1, MID) as i:
                feed(i)
            load_pair(2 * MID, 0)
            store_max(2 * MID - 1, 1)
            store_max(2 * MID, 0)

            def two_load(t, k):
                sp.dma_start(xt[k], xs_d[bass.ds(t * P, 2 * P), :].rearrange("(u p) d -> p u d", p=P)
                             ).then_inc(xt_in[k], 16)

            def two_store(i, j):
                t = BODY * i + j
                sp.wait_ge(y_ok, t + 2)
                sp.dma_start(ys_d[bass.ds(t * P, 2 * P), :].rearrange("(u p) d -> p u d", p=P),
                             ys[j // 2 % 2]).then_inc(y_out[j // 2 % 2], 16)

            def expert_io(i, first):
                for j in range(0, BODY, 2):
                    t = BODY * i + j
                    sp.wait_ge(xt_tr, t + 2)
                    two_load(t + 4, j // 2 % 2)
                    if not (first and j < 4):
                        two_store(i, j - 4)

            sp.wait_ge(scattered, 16 * 2 * T)
            for k in range(2):
                two_load(2 * k, k)
            expert_io(0, True)
            for side in range(2):
                for i, j in ((i, j) for i in range(PARTS) for j in range(PARTS)):
                    load_rows(2 * MID + 1, 1, side, i, j)
                expert_io(1 + side, False)
            with sp.Fori(3, SLOT_TILES // BODY) as i:
                expert_io(i, False)
            two_store(SLOT_TILES // BODY, -4)
            two_store(SLOT_TILES // BODY, -2)

            with sp.Fori(MID + 1, ITERS) as i:
                feed(i)
            store_max(PAIRS - 1, 1)

            for g in range(T // G):
                sp.wait_ge(fin_ok, g + 1)
                b, t = g * G // TB, g * G % TB
                sp.dma_start(out_d[b, t * P:(t + G) * P, :].rearrange("(t p) d -> p t d", p=P),
                             fin[g % 2]).then_inc(fin_out[g % 2], 16)
            for k in range(2):
                sp.wait_ge(fin_out[k], 16 * T // G // 2)

        @block.gpsimd
        def _(pool):
            nc.gpsimd.memset(xh[:, :, :], 0.0).then_inc(slots_zero, 1)
            pool.wait_ge(slots_zero, 1)
            for t in range(0, XS_TILES, T):
                n = min(T, XS_TILES - t)
                pool.dma_start(xs_d[t * P:(t + n) * P, :].rearrange("(t p) d -> p t d", p=P),
                               xh[:, 0:n, :]).then_inc(zeroed, 16)
            for k in range(2):
                v = v_aug[k]
                nc.gpsimd.memset(v[:, :, :, :], 0.0).then_inc(v_zero, 1)
            pool.wait_ge(v_zero, 2)
            for k in range(2):
                nc.gpsimd.memset(v_aug[k][:, :, :, DK:DK + 1], 1.0).then_inc(v_one, 1)
            pool.wait_ge(v_one, 2)
            for k in range(2):
                nc.gpsimd.memset(qs[k][64:96, :, :], 0.0).then_inc(stack_ok, 1)
                nc.gpsimd.memset(ks[k][64:96, :, :], 1.0).then_inc(stack_ok, 1)

            def low(n):
                pool.wait_ge(mid_ok, n + 1)
                nc.gpsimd.tensor_tensor(part[:, n % PR, 2, :], prod_c[n % 4], part[:, n % PR, 1, :], ALU.subtract
                                        ).then_inc(lo_ok, 1)

            pool.wait_ge(stack_ok, 4)
            for n in range(STEPS):
                pool.wait_ge(rope_out, 2 * (n + 1))
                nc.gpsimd.tensor_tensor(prod_c[n % 4], prod_c[n % 4], prod_s[n % 4], ALU.add).then_inc(rope_sum, 1)
                if n >= 2:
                    low(n - 2)
            low(STEPS - 2)
            low(STEPS - 1)
            pool.wait_ge(xn_ok, T)
            pool.wait_ge(xh_scale, 1)
            pool.wait_ge(zeroed, 48)
            for t in range(T):
                nc.gpsimd.tensor_scalar(xh[:, t, :], xn[:, t, :], small[:, 7, t:t + 1], None,
                                        ALU.mult).then_inc(xh_ok, 1)

            pool.wait_ge(slot_ok, 2)
            pool.wait_ge(xh_ok, T)
            for t in range(T):
                for k in range(2):
                    pool.indirect_dma_start(out=xs_d[:, :],
                                            out_offset=bass.IndirectOffsetOnAxis(ap=slot[:, k, t:t + 1], axis=0),
                                            in_=xh[:, t, :], in_offset=None).then_inc(scattered, 16)

            for k in range(2):
                pool.wait_ge(y_out[k], 16 * SLOT_TILES // 4)
            pool.wait_ge(base_ok, T)
            for t in range(T):
                for k, dst in ((0, xn), (1, xh)):
                    pool.indirect_dma_start(out=dst[:, t, :], out_offset=None, in_=ys_d[:, :],
                                            in_offset=bass.IndirectOffsetOnAxis(ap=slot[:, k, t:t + 1], axis=0)
                                            ).then_inc(gathered, 16)

        @block.tensor
        def _(pe):
            pe.wait_ge(const_in, 16)
            pe.wait_ge(w_in, 64)
            for k in range(4):
                last = nc.tensor.transpose(sc[0][:, k * D:(k + 1) * D], wr[:, k, :], ident)
            last.then_inc(wtr, 1)

            def head_norms(n):
                b, c, s = n // 4, n // 2 % 2, n % 2
                pe.wait_ge(sq_ok, n + 1)
                wait(pe, norm_in, b)
                j = 32 * (2 * s + c)
                nc.tensor.matmul(acc[1][j:j + 32, :], head_of[:, :], square[s][:, :], start=True,
                                 stop=True).then_inc(norm_mm, 1)

            pe.wait_ge(head_ok, 1)
            pe.wait_ge(wtr_out, 6)
            pe.wait_ge(gate_in, 16)

            def turn(m):
                pe.wait_ge(xn_ok, HALF * (m + 1))
                wait(pe, xtr_out, m - 1)
                for u in range(HALF):
                    last = nc.tensor.transpose(sc[2][:, (m % 2) * CH + u * P:(m % 2) * CH + (u + 1) * P],
                                               xn[:, m * HALF + u, :], ident)
                last.then_inc(xtr, 1)

            def values(n):
                wait(pe, v_out, 2 * n)
                for u in range(2):
                    t = 2 * n + u
                    last = nc.tensor.matmul(acc[0][:, u * (D + E):(u + 1) * (D + E)],
                                            xnT[:, t * P:(t + 1) * P], wvg[:, :], start=True, stop=True)
                last.then_inc(v_mm, 1)

            turn(0)
            turn(1)
            for n in range(STEPS):
                m, s = n // 2, n % 2
                if s == 0 and 2 <= m + 1 < 2 * B:
                    turn(m + 1)
                pe.wait_ge(xtr_out, m + 1)
                wait(pe, rope_out, 2 * (n - 1))
                for r in range(2):
                    last = nc.tensor.matmul(sc[s][:, r * CH:(r + 1) * CH], wT[:, 2 * s + r, :],
                                            xnT[:, m * CH:(m + 1) * CH], start=True, stop=True)
                last.then_inc(proj, 1)
                if n == 1:
                    pe.wait_ge(rows_in, 48)
                    nc.tensor.transpose(acc[1][:, 0:48], rows[0:48, :], ident[0:48, 0:48]).then_inc(rtr, 1)
                if n == 2:
                    pe.wait_ge(rtr_out, 3)
                if n >= 2:
                    head_norms(n - 2)
                if n < STEPS - LATE:
                    values(n)
            for n in range(STEPS - LATE, STEPS):
                values(n)
                head_norms(n)

            pe.wait_ge(norm_in, B)
            nc.tensor.transpose(acc[1][0:B, 0:P], norms[:, :], ident).then_inc(bound_tr, 1)
            pe.wait_ge(bound_ok, 1)
            nc.tensor.transpose(acc[1][0:1, P:P + B], norm_m[:, :], ident[0:B, 0:B]).then_inc(bound_tr2, 1)
            pe.wait_ge(flag_ok, 1)
            fast = pe.value_load(flag[0:1, 0:1], min_val=0, max_val=1)

            def scores(k, u, a, kb):
                for half in range(2):
                    last = nc.tensor.matmul(sc[u][:, half * CH:(half + 1) * CH], ks[k][0:KR, a, kb * P:(kb + 1) * P],
                                            qs[k][0:KR, a, half * CH:(half + 1) * CH], start=True, stop=True)
                last.then_inc(s_mm, 1)

            def maxima(p, k):
                wait(pe, e_ok, 16 * p)
                for n in range(2 * TB):
                    a, q = n // TB, n % TB
                    if n >= 2:
                        pe.wait_ge(m_red, 16 * p + n - 1)
                    for half in range(2):
                        last = nc.tensor.matmul(sc[n % 2][:, half * CH:(half + 1) * CH],
                                                qs[k][0:ROWS, a, q * P:(q + 1) * P],
                                                ks[k][0:ROWS, a, half * CH:(half + 1) * CH], start=True, stop=True)
                    last.then_inc(m_mm, 1)
                pe.wait_ge(m_red, 16 * (p + 1))
                nc.tensor.transpose(sc[2][0:2 * TB, 0:P], mx[:, :], ident).then_inc(m_tr, 1)
                pe.wait_ge(m_in, 48 * (p + 1))

            def enter_pair(i, k):
                p = 2 * i + k
                pe.wait_ge(qk_in[k], 16 * LOADS * (i + 1))
                with pe.If(fast == 0):
                    maxima(p, k)

            def untangle(p, k, c):
                if c == 0:
                    pe.wait_ge(acc_ok, p + 1)
                tr = nc.tensor.transpose(acc[k][:, c * P:(c + 1) * P], acc_s[:, c * P:(c + 1) * P], ident)
                if c == 3:
                    tr.then_inc(acc_tr, 1)

            def ranks():
                pe.wait_ge(pick_ok, 1)
                nc.tensor.matmul(acc[1][:, 0:T * E], before, cnt[:, 0, :, :], start=True, stop=True)
                nc.tensor.matmul(acc[1][:, T * E:2 * T * E], ones, cnt[:, 0, :, :], start=True,
                                 stop=True).then_inc(rank_mm, 1)
                pe.wait_ge(rank_ok, 1)

            def attend(i, first, last_iter):
                for s in range(2 * KB):
                    k, kb = s // KB, s % KB
                    p = 2 * i + k
                    if s + 1 < 2 * KB or not last_iter:
                        nk, nkb = ((s + 1) // KB) % 2, (s + 1) % KB
                        if nkb == 0:
                            enter_pair(i + (s + 1) // (2 * KB), nk)
                        for a in range(2):
                            u = 2 * (s + 1) + a
                            if s + 1 == 2 * KB:
                                pe.wait_ge(e_ok, 32 * i + 31 + a)
                                scores(nk, a, a, nkb)
                            else:
                                if u >= 3 and a == 1:
                                    pe.wait_ge(e_ok, 32 * i + u - 2)
                                scores(nk, u % 3, a, nkb)
                    if kb == 0:
                        if first and k == 1:
                            ranks()
                        pe.wait_ge(v_ok, p + 1)
                        if not (first and k == 0):
                            wait(pe, norm_ok, p - 1)
                    pe.wait_ge(e_ok, 32 * i + 2 * s + 2)
                    for a in range(2):
                        for half in range(2):
                            j = 2 * a + half
                            mm = nc.tensor.matmul(acc[k][32 * j:32 * j + 32, :], v_aug[k][:, kb, a, :],
                                                  probs[(2 * s + a) % 4][:, half, :],
                                                  start=(kb == 0), stop=(kb == KB - 1))
                    mm.then_inc(pv_mm, 1)
                    if 1 <= kb <= 4 and not (first and k == 0):
                        untangle(p - 1, 1 - k, kb - 1)

            enter_pair(0, 0)
            for a in range(2):
                scores(0, a, a, 0)
            attend(0, True, False)
            with pe.Fori(1, MID) as i:
                attend(i, False, False)

            def tile_in(i, j):
                if j % 2 == 0:
                    pe.wait_ge(xt_in[j // 2 % 2], 16 * (BODY // 4 * i + j // 4 + 1))
                nc.tensor.transpose(sc[2][:, (j % 2) * CH:(j % 2) * CH + P], xt[j // 2 % 2][:, j % 2, :], ident
                                    ).then_inc(xt_tr, 1)

            def layer_one(t, j):
                pe.wait_ge(xsT_ok, t + 1)
                for c in range(FC):
                    mm = nc.tensor.matmul(sc[0][:, (j % 2) * CH + c * P:(j % 2) * CH + (c + 1) * P],
                                          w_tile[j % 4][:, c * P:(c + 1) * P], xsT[j % 2],
                                          start=True, stop=True)
                mm.then_inc(h_mm, 1)

            def layer_two(t, j):
                pe.wait_ge(relu_ok, t + 1)
                for c in range(FC):
                    mm = nc.tensor.matmul(sc[1][:, (j % 2) * CH:(j % 2) * CH + D], hT[j % 2][:, c, :],
                                          w_tile[j % 4][:, W2_AT + c * D:W2_AT + (c + 1) * D],
                                          start=(c == 0), stop=(c == FC - 1))
                mm.then_inc(y_mm, 1)

            def expert_body(i, first):
                for j in range(BODY):
                    t = BODY * i + j
                    tile_in(i, j + 1)
                    layer_one(t, j)
                    if not (first and j == 0):
                        layer_two(t - 1, j + BODY - 1)

            pe.wait_ge(e_ok, 32 * MID + 2)
            tile_in(0, 0)
            expert_body(0, True)
            with pe.Fori(1, SLOT_TILES // BODY) as i:
                expert_body(i, False)
            pe.wait_ge(y_ok, SLOT_TILES - 2)
            layer_two(SLOT_TILES - 1, BODY - 1)

            pe.wait_ge(y_ok, SLOT_TILES)
            pe.wait_ge(xsT_ok, SLOT_TILES + 1)
            with pe.Fori(MID, ITERS - 1) as i:
                attend(i, False, False)
            attend(ITERS - 1, False, True)

            def project(g):
                pe.wait_ge(oT_ok, g + 1)
                wait(pe, fin_ok, g - 1)
                for n in range(G):
                    mm = nc.tensor.matmul(sc[1][:, (g % 2) * CH + n * D:(g % 2) * CH + (n + 1) * D],
                                          oT[g % 2][:, n, :], woT[:, :], start=True, stop=True)
                mm.then_inc(o_mm, 1)

            for g in range(T // G):
                if g == LAST_GROUPS:
                    pe.wait_ge(norm_ok, PAIRS)
                wait(pe, oT_ok, g - 1)
                for n in range(G):
                    t = g * G + n
                    last = nc.tensor.transpose(sc[0][:, (g % 2) * CH + n * P:(g % 2) * CH + (n + 1) * P],
                                               att[:, t // TB, t % TB, :], ident)
                last.then_inc(o_tr, 1)
                if g == 0:
                    for c in range(4):
                        untangle(PAIRS - 1, 1, c)
                else:
                    project(g - 1)
            project(T // G - 1)

        @block.scalar
        def _(act):
            act.dma_start(const[:, :], const_d).then_inc(const_in, 16)
            for k, w in enumerate((wq_d, wk_d)):
                act.dma_start(wr[:, k, :], w).then_inc(w_in, 16)

            def roots(g):
                ts, k = ln_tiles[g], g // 2
                act.wait_ge(ln_var, g + 1)
                nc.scalar.activation(small[:, 9 + k, ts], small[:, 3 + 2 * k, ts], ACT.Sqrt).then_inc(ln_sqrt, 1)

            def layernorm(t):
                act.wait_ge(ln_ok, 1 if t < TB else 2)
                nc.scalar.activation(xn[:, t, :], x[:, t, :], ACT.Identity, scale=small[:, 6, t:t + 1],
                                     bias=small[:, 8, t:t + 1]).then_inc(xn_ok, 1)

            def high(n):
                act.wait_ge(rope_sum, n + 1)
                wait(act, part_out[n % PR], 16 * PARTS * (n // PR))
                nc.scalar.copy(part[:, n % PR, 0, :], prod_c[n % 4]).then_inc(hi_ok, 1)

            def squares(n):
                wait(act, norm_mm, n - 1)
                nc.scalar.activation(square[n % 2][:, :], prod_c[n % 4], ACT.Square).then_inc(sq_ok, 1)

            def middle(n):
                act.wait_ge(mid_in, n + 1)
                nc.scalar.copy(part[:, n % PR, 1, :], prod_c[n % 4]).then_inc(mid_ok, 1)

            def columns(m):
                act.wait_ge(xtr, m + 1)
                nc.scalar.copy(xnT[:, m * CH:(m + 1) * CH], sc[2][:, (m % 2) * CH:(m % 2 + 1) * CH]
                               ).then_inc(xtr_out, 1)

            roots(0)
            for t in range(TB):
                layernorm(t)
            columns(0)
            columns(1)
            roots(1)
            ahead = TB + HALF
            for t in range(TB, ahead):
                layernorm(t)
            for n in range(STEPS):
                if n % 2 == 0 and 2 <= n // 2 + 1 < 2 * B:
                    columns(n // 2 + 1)
                high(n)
                squares(n)
                if n >= 1:
                    middle(n - 1)
                if n == SECOND + 1:
                    roots(2)
                for t in range(ahead + 2 * n, min(ahead + 2 * n + 2, T)):
                    layernorm(t)
            middle(STEPS - 1)

            def exp_unit(i, u):
                act.wait_ge(s_mm, 32 * i + u + 1)
                nc.scalar.activation(probs[u % 4], sc[u % 3][:, :].rearrange("p (h c) -> p h c", h=2),
                                     ACT.Exp, scale=SCALE).then_inc(e_ok, 1)

            def attend(i, first):
                for u in range(4 * KB):
                    exp_unit(i, u)
                    if first and u == 2 * KB - 1:
                        act.wait_ge(gap_ok, 1)
                        nc.scalar.activation(small[:, 1, :], small[:, 0, :], ACT.Exp).then_inc(gate_exp, 1)

            nc.scalar.activation(small[:, 1, 0:1], ident[:, 0:1], ACT.Exp).then_inc(table_in, 1)
            act.wait_ge(table_in, 1)
            act.wait_ge(flag_ok, 1)
            act.wait_ge(lo_ok, STEPS)
            attend(0, True)
            with act.Fori(1, MID) as i:
                attend(i, False)

            exp_unit(MID, 0)
            exp_unit(MID, 1)

            def relu(i, j):
                t = BODY * i + j
                act.wait_ge(h_mm, t + 1)
                for c in range(FC):
                    a = nc.scalar.activation(hT[j % 2][:, c, :], sc[0][:, (j % 2) * CH + c * P:
                                                                       (j % 2) * CH + (c + 1) * P],
                                             ACT.Relu, bias=w_tile[j % 4][:, B1_AT + c:B1_AT + c + 1])
                a.then_inc(relu_ok, 1)

            for j in range(BODY):
                relu(0, j)
            with act.Fori(1, SLOT_TILES // BODY) as i:
                for j in range(BODY):
                    relu(i, j)

            for u in range(2, 4 * KB):
                exp_unit(MID, u)
            with act.Fori(MID + 1, ITERS) as i:
                attend(i, False)

            for g in range(T // G):
                act.wait_ge(o_tr, g + 1)
                wait(act, o_mm, g - 1)
                nc.scalar.copy(oT[g % 2], sc[0][:, (g % 2) * CH:(g % 2 + 1) * CH].rearrange("p (t c) -> p t c", t=G)
                               ).then_inc(oT_ok, 1)

        @block.vector
        def _(v):
            chain = [0]
            counted, spare = [0], [False]

            def row_moments():
                t = counted[0]
                if t < T:
                    if t % TB == 0:
                        v.wait_ge(x_in[t // TB], 16)
                    counted[0] = t + 1
                    return nc.vector.bn_stats(stats[:, t, :], x[:, t, :])

            def link(ins):
                chain[0] += 1
                ins.then_inc(dve, 1)
                if spare[0]:
                    row_moments()
                v.wait_ge(dve, chain[0])

            nc.vector.memset(ones, 1.0)

            def layernorm_factors(g):
                ts = ln_tiles[g]
                while counted[0] < ts.stop:
                    last = row_moments()
                link(last)
                for t in range(ts.start, ts.stop):
                    last = nc.vector.bn_aggr(mv[:, t, :], stats[:, t, :])
                link(last)
                spare[0] = g == 0
                mean, var = mv[:, ts, 0], mv[:, ts, 1]

                link(nc.vector.tensor_scalar(small[:, 2, ts], var, 1e-5, None, ALU.add))
                nc.vector.reciprocal(small[:, 3, ts], small[:, 2, ts]).then_inc(ln_var, 1)
                link(newton(g, 0, 6))
                rstd = small[:, 6, ts]
                link(nc.vector.tensor_tensor(small[:, 8, ts], mean, rstd, ALU.mult))
                nc.vector.tensor_scalar(small[:, 8, ts], small[:, 8, ts], -1.0, None, ALU.mult).then_inc(ln_ok, 1)

            def newton(g, k, dst):
                ts = ln_tiles[g]
                y0, tmp, val = small[:, 9 + k, ts], small[:, 11, ts], small[:, 2 + 2 * k, ts]
                v.wait_ge(ln_sqrt, g + 1)
                link(nc.vector.tensor_tensor(tmp, y0, y0, ALU.mult))
                link(nc.vector.tensor_tensor(tmp, tmp, val, ALU.mult))
                link(nc.vector.tensor_scalar(tmp, tmp, -0.5, 1.5, ALU.mult, ALU.add))
                return nc.vector.tensor_tensor(small[:, dst, ts], y0, tmp, ALU.mult)

            def expert_variance():
                rstd = small[:, 6, :]
                link(nc.vector.tensor_tensor(small[:, 4, :], mv[:, :, 1], rstd, ALU.mult))
                link(nc.vector.tensor_tensor(small[:, 4, :], small[:, 4, :], rstd, ALU.mult))
                link(nc.vector.tensor_scalar(small[:, 4, :], small[:, 4, :], 1e-6, None, ALU.add))
                nc.vector.reciprocal(small[:, 5, :], small[:, 4, :]).then_inc(ln_var, 1)

            layernorm_factors(0)
            spare[0] = False

            v.wait_ge(wtr, 1)
            ps = sc[0][:, 0:4 * D].rearrange("p (k d) -> p k d", k=4)
            for s in range(2):
                nc.vector.tensor_copy(wT[:, 2 * s, :], ps[:, s, :]).then_inc(wtr_out, 1)
                two = ps[:, s, :].rearrange("p (i r) -> p i r", r=2)
                rot = wT[:, 2 * s + 1, :].rearrange("p (i r) -> p i r", r=2)
                nc.vector.tensor_scalar(rot[:, :, 0], two[:, :, 1], -1.0, None, ALU.mult)
                nc.vector.tensor_copy(rot[:, :, 1], two[:, :, 0]).then_inc(wtr_out, 1)
            nc.vector.tensor_copy(wvg[:, 0:D], ps[:, 2, :]).then_inc(wtr_out, 1)
            nc.vector.tensor_copy(woT[:, :], ps[:, 3, :]).then_inc(wtr_out, 1)
            nc.vector.tensor_copy(head_of[:, :], head_row).then_inc(head_ok, 1)

            layernorm_factors(1)

            v.wait_ge(rope_in, 32)

            def rotate(n):
                c, s = n // 2 % 2, n % 2
                v.wait_ge(proj, n + 1)
                wait(v, lo_ok, n - 3)
                pos = slice(c * CH, (c + 1) * CH)
                nc.vector.tensor_tensor(prod_c[n % 4], sc[s][:, 0:CH], cos[:, pos], ALU.mult).then_inc(rope_out, 1)
                nc.vector.tensor_tensor(prod_s[n % 4], sc[s][:, CH:2 * CH], sin[:, pos], ALU.mult
                                        ).then_inc(rope_out, 1)

            def rest(n):
                v.wait_ge(hi_ok, n + 1)
                v.wait_ge(sq_ok, n + 1)
                nc.vector.tensor_tensor(prod_c[n % 4], prod_c[n % 4], part[:, n % PR, 0, :], ALU.subtract
                                        ).then_inc(mid_in, 1)

            def values(n):
                v.wait_ge(v_mm, n + 1)
                src = acc[0][:, 0:2 * (D + E)].rearrange("p (t c) -> p t c", t=2)
                b, t = 2 * n // TB, 2 * n % TB
                nc.vector.tensor_copy(v_all[:, b * PB:(b + 1) * PB, t:t + 2, :].rearrange("p a t w -> p t a w"),
                                      src[:, :, 0:D].rearrange("p t (a w) -> p t a w", a=PB)).then_inc(v_out, 1)
                nc.vector.tensor_copy(score[:, 2 * n:2 * n + 2, :], src[:, :, D:D + E]).then_inc(v_out, 1)

            def batch_norms(b):
                v.wait_ge(norm_mm, 4 * (b + 1))
                nc.vector.reduce_max(norms[:, b:b + 1], acc[1][:, :], AX.X).then_inc(norm_in, 1)

            for n in range(STEPS):
                rotate(n)
                if n >= 5 and n % 4 == 1:
                    batch_norms((n - 5) // 4)
                if n >= 1:
                    rest(n - 1)
                if n < STEPS - LATE:
                    values(n)
                if n == SECOND:
                    expert_variance()
                if n == 1:
                    v.wait_ge(rtr, 1)
                    nc.vector.tensor_copy(w_all[:, :, B1_AT:B1_AT + FC],
                                          acc[1][:, 0:32].rearrange("p (e c) -> p e c", e=E)).then_inc(rtr_out, 1)
                    nc.vector.tensor_copy(w_all[:, :, GA_AT], acc[1][:, 32:40]).then_inc(rtr_out, 1)
                    nc.vector.tensor_copy(w_all[:, :, BE_AT], acc[1][:, 40:48]).then_inc(rtr_out, 1)
            for n in range(STEPS - LATE, STEPS):
                values(n)
            batch_norms(B - 1)
            rest(STEPS - 1)

            v.wait_ge(bound_tr, 1)
            rows4 = acc[1][0:B, 0:P].rearrange("b (s c h) -> b s c h", s=2, c=2)
            for k in range(2):
                last = nc.vector.reduce_max(norm_b[:, k, :], rows4[:, k, :, 0:H].rearrange("b c h -> b h c"), AX.X)
            link(last)
            link(nc.vector.tensor_tensor(norm_b[:, 2, :], norm_b[:, 0, :], norm_b[:, 1, :], ALU.mult))
            nc.vector.reduce_max(norm_m[:, :], norm_b[:, 2, :], AX.X).then_inc(bound_ok, 1)
            v.wait_ge(bound_tr2, 1)
            link(nc.vector.reduce_max(flag_f[:, 0, :], acc[1][0:1, P:P + B], AX.X))
            nc.vector.tensor_scalar(flag[:, :], flag_f[:, 0, :], (SAFE / SCALE) ** 2, None, ALU.is_le
                                    ).then_inc(flag_ok, 1)

            v.wait_ge(flag_ok, 1)
            fast = v.value_load(flag[0:1, 0:1], min_val=0, max_val=1)
            newton(2, 1, 7).then_inc(xh_scale, 1)

            def maxima(p):
                for n in range(2 * TB):
                    v.wait_ge(m_mm, 16 * p + n + 1)
                    nc.vector.reduce_max(mx[:, n:n + 1], sc[n % 2][:, :], AX.X).then_inc(m_red, 1)
                v.wait_ge(m_tr, p + 1)
                wait(v, m_in, 48 * p)
                base = 5 * p
                nc.vector.tensor_scalar(mrow[:, 0, :], sc[2][0:2 * TB, 0:P], -1.0, None, ALU.mult).then_inc(m_chain, 1)
                v.wait_ge(m_chain, base + 1)
                nc.vector.tensor_copy(mpart[:, 0, :], mrow[:, 0, :]).then_inc(m_chain, 1)
                v.wait_ge(m_chain, base + 2)
                nc.vector.tensor_tensor(mrow[:, 1, :], mrow[:, 0, :], mpart[:, 0, :], ALU.subtract
                                        ).then_inc(m_chain, 1)
                v.wait_ge(m_chain, base + 3)
                nc.vector.tensor_copy(mpart[:, 1, :], mrow[:, 1, :]).then_inc(m_chain, 1)
                v.wait_ge(m_chain, base + 4)
                nc.vector.tensor_tensor(mrow[:, 2, :], mrow[:, 1, :], mpart[:, 1, :], ALU.subtract
                                        ).then_inc(m_chain, 1)
                v.wait_ge(m_chain, base + 5)
                nc.vector.tensor_copy(mpart[:, 2, :], mrow[:, 2, :]).then_inc(m_split, 1)

            def normalise(p, k):
                v.wait_ge(acc_tr, p + 1)
                ps = acc[k][:, :].rearrange("p (c a h w) -> p c a h w", c=4, a=2, h=2)
                for a in range(2):
                    nc.vector.reciprocal(rec[:, 2 * a:2 * a + 2, :], ps[:, :, a, :, DK].rearrange("p c h -> p h c")
                                         ).then_inc(rec_ok, 1)
                v.wait_ge(rec_ok, 2 * (p + 1))
                for a in range(2):
                    for h in range(2):
                        dst = att[:, bass.ds(p // PB, 1), 4 * h:4 * h + 4,
                                  bass.ds((p % PB) * 2 * DK + a * DK, DK)]
                        m = nc.vector.tensor_tensor(dst.rearrange("p o c d -> p (o c) d"), ps[:, :, a, h, 0:DK],
                                                    rec[:, 2 * a + h, :].unsqueeze(2).to_broadcast([P, 4, DK]),
                                                    ALU.mult)
                m.then_inc(norm_ok, 1)

            def take(p, k):
                v.wait_ge(pv_mm, 8 * (p + 1))
                nc.vector.tensor_copy(acc_s[:, :], acc[k][:, :]).then_inc(acc_ok, 1)

            def route():
                for t in range(T):
                    last = nc.vector.max(top[:, t, :], score[:, t, :])
                link(last)
                for t in range(T):
                    last = nc.vector.max_index(topi[:, t, :], top[:, t, :], score[:, t, :])
                link(last)
                nc.vector.tensor_tensor(small[:, 0, :], top[:, :, 1], top[:, :, 0], ALU.subtract).then_inc(gap_ok, 1)
                link(nc.vector.tensor_copy(topf[:, :, :], topi[:, :, 0:2]))
                for k in range(2):
                    link(nc.vector.tensor_tensor(pick[:, k, :, :], iota_e.unsqueeze(1).to_broadcast([P, T, E]),
                                                 topf[:, :, k:k + 1].to_broadcast([P, T, E]), ALU.is_equal))
                nc.vector.tensor_tensor(cnt[:, 0, :, :], pick[:, 0, :, :], pick[:, 1, :, :], ALU.add
                                        ).then_inc(pick_ok, 1)

            def take_ranks():
                v.wait_ge(rank_mm, 1)
                nc.vector.tensor_copy(rank[:, :, :, :], acc[1][:, :].rearrange("p (a t e) -> p a t e", a=2, e=E)
                                      ).then_inc(rank_ok, 1)

            def place():
                v.wait_ge(gate_exp, 1)
                e, w1, w2, ws = small[:, 1, :], small[:, 2, :], small[:, 3, :], small[:, 4, :]
                link(nc.vector.tensor_scalar(w2, e, 1.0, None, ALU.add))
                link(nc.vector.reciprocal(w1, w2))
                link(nc.vector.tensor_tensor(w2, e, w1, ALU.mult))
                link(nc.vector.tensor_tensor(ws, w1, w2, ALU.add))

                v.wait_ge(rank_ok, 1)
                link(nc.vector.tensor_copy(cnt[:, 1, :, :], rank[:, 1, :, :]))
                a, shift = 1, 1
                while shift < T:
                    nxt = 3 - a
                    nc.vector.tensor_copy(cnt[:, nxt, 0:shift, :], cnt[:, a, 0:shift, :])
                    link(nc.vector.tensor_tensor(cnt[:, nxt, shift:T, :], cnt[:, a, shift:T, :],
                                                 cnt[:, a, 0:T - shift, :], ALU.add))
                    a, shift = nxt, 2 * shift
                incl = cnt[:, a, :, :]
                total = incl[:, T - 1, :]
                link(nc.vector.tensor_scalar(exp_s[:, 0, :], total, float(P - 1), None, ALU.add))
                link(nc.vector.tensor_copy(exp_i[:, 0, :], exp_s[:, 0, :]))
                link(nc.vector.tensor_scalar(exp_i[:, 1, :], exp_i[:, 0, :], 7, None, ALU.arith_shift_right))
                link(nc.vector.tensor_copy(exp_s[:, 0, :], exp_i[:, 1, :]))
                link(nc.vector.tensor_copy(exp_s[:, 1, :], exp_s[:, 0, :]))
                a2, shift = 1, 1
                while shift < E:
                    nxt = 3 - a2
                    nc.vector.tensor_copy(exp_s[:, nxt, 0:shift], exp_s[:, a2, 0:shift])
                    link(nc.vector.tensor_tensor(exp_s[:, nxt, shift:E], exp_s[:, a2, shift:E],
                                                 exp_s[:, a2, 0:E - shift], ALU.add))
                    a2, shift = nxt, 2 * shift
                ends = exp_s[:, a2, :]
                link(nc.vector.tensor_tensor(exp_s[:, 3, :], ends, exp_s[:, 0, :], ALU.subtract))
                link(nc.vector.tensor_scalar(exp_s[:, 3, :], exp_s[:, 3, :], float(P), None, ALU.mult))
                pos = cnt[:, 3, :, :]
                link(nc.vector.tensor_tensor(pos, incl, rank[:, 1, :, :],
                                             ALU.subtract))
                link(nc.vector.tensor_tensor(pos, pos, rank[:, 0, :, :], ALU.add))
                link(nc.vector.tensor_tensor(pos, pos, exp_s[:, 3:4, :].to_broadcast([P, T, E]), ALU.add))
                for k in range(2):
                    link(nc.vector.tensor_tensor(cnt[:, 0, :, :], pos, pick[:, k, :, :], ALU.mult))
                    link(nc.vector.reduce_sum(slot_f[:, k, :], cnt[:, 0, :, :], AX.X))
                    nc.vector.tensor_copy(slot[:, k, :], slot_f[:, k, :]).then_inc(slot_ok, 1)
                own_cmp = cnt[0:1, :, :, :].rearrange("p a t e -> p (a t) e")[:, 0:SLOT_TILES + 2, :]
                link(nc.vector.tensor_tensor(own_cmp,
                                             iota_t[0:1, :].unsqueeze(2).to_broadcast([1, SLOT_TILES + 2, E]),
                                             exp_s[0:1, a2:a2 + 1, :].to_broadcast([1, SLOT_TILES + 2, E]), ALU.is_ge))
                link(nc.vector.reduce_sum(owner_f[:, 0, :], own_cmp, AX.X))
                link(nc.vector.tensor_scalar(owner_f[:, 1, :], owner_f[:, 0, :], float(E - 1), None, ALU.min))
                nc.vector.tensor_copy(owner[:, :], owner_f[:, 1, :]).then_inc(owner_ok, 1)


            def residuals():
                v.wait_ge(xh_ok, T)
                for t in range(T):
                    nc.vector.scalar_tensor_tensor(out=x[:, t, :], in0=xn[:, t, :], scalar=small[:, 4, t:t + 1],
                                                   in1=x[:, t, :], op0=ALU.mult, op1=ALU.add).then_inc(base_ok, 1)

            def copy_v(p, k):
                wait(v, pv_mm, 8 * (p - 1))
                nc.vector.tensor_copy(v_aug[k][:, :, :, 0:DK],
                                      v_all[:, bass.ds(p, 1), :, :].rearrange("p o k (a d) -> p (o k) a d", a=2)
                                      ).then_inc(v_ok, 1)

            def attend(i, last_iter, before_take, after_take):
                for k in range(2):
                    p = 2 * i + k
                    if not isinstance(p, int) or p > 0:
                        normalise(p - 1, 1 - k)
                    if not (last_iter and k == 1):
                        copy_v(p + 1, 1 - k)
                    if before_take[k]:
                        before_take[k]()
                    if not (last_iter and k == 1):
                        with v.If(fast == 0):
                            maxima(p + 1)
                    take(p, k)
                    if after_take[k]:
                        after_take[k]()

            with v.If(fast == 0):
                maxima(0)
            nothing = (None, None)
            v.wait_ge(v_one, 2)
            v.wait_ge(v_out, 2 * STEPS)
            copy_v(0, 0)
            attend(0, False, (route, None), (take_ranks, place))
            attend(1, False, nothing, (residuals, None))

            v.wait_ge(exp_in, 16 * 3 * E)

            def weights(t, j):
                e = v.value_load(owner[0:1, bass.ds(t, 1)], min_val=0, max_val=E - 1)
                wait(v, y_ok, t - 3)
                nc.vector.tensor_copy(w_tile[j % 4],
                                      w_all[:, bass.ds(e, 1), :].rearrange("p o w -> p (o w)")).then_inc(w_ok, 1)

            weights(0, 0)
            weights(1, 1)
            with v.Fori(2, MID) as i:
                attend(i, False, nothing, nothing)

            def columns(t, j):
                v.wait_ge(xt_tr, t + 1)
                v.wait_ge(w_ok, t + 1)
                nc.vector.tensor_scalar(xsT[j % 2], sc[2][:, (j % 2) * CH:(j % 2) * CH + P],
                                        w_tile[j % 4][:, GA_AT:GA_AT + 1], w_tile[j % 4][:, BE_AT:BE_AT + 1],
                                        ALU.mult, ALU.add).then_inc(xsT_ok, 1)

            def rows_out(i, j):
                t = BODY * i + j
                v.wait_ge(y_mm, t + 1)
                if j % 2 == 0:
                    wait(v, y_out[j // 2 % 2], 16 * (BODY // 4 * i + j // 4))
                nc.vector.tensor_tensor(ys[j // 2 % 2][:, j % 2, :], sc[1][:, (j % 2) * CH:(j % 2) * CH + D],
                                        w_tile[j % 4][:, B2_AT:B2_AT + D], ALU.add).then_inc(y_ok, 1)

            def expert_body(i, first):
                for j in range(BODY):
                    t = BODY * i + j
                    if not (first and j < 2):
                        rows_out(i, j - 2)
                    columns(t + 1, j + 1)
                    weights(t + 2, j + 2)

            columns(0, 0)
            expert_body(0, True)
            with v.Fori(1, SLOT_TILES // BODY) as i:
                expert_body(i, False)
            rows_out(SLOT_TILES // BODY - 1, BODY - 2)
            rows_out(SLOT_TILES // BODY - 1, BODY - 1)

            def merge(group):
                def add():
                    v.wait_ge(gathered, 16 * 2 * T)
                    for src, wk in ((xn, 2), (xh, 3)):
                        for t in range(group * 4, group * 4 + 4):
                            last = nc.vector.scalar_tensor_tensor(out=x[:, t, :], in0=src[:, t, :],
                                                                  scalar=small[:, wk, t:t + 1], in1=x[:, t, :],
                                                                  op0=ALU.mult, op1=ALU.add)
                        link(last)
                return add

            with v.Fori(MID, MERGE[0]) as i:
                attend(i, False, nothing, nothing)
            for i in range(*MERGE):
                n = 2 * (i - MERGE[0])
                attend(i, False, nothing, (merge(n), merge(n + 1)))
            attend(ITERS - 1, True, nothing, nothing)
            normalise(PAIRS - 1, 1)

            for g in range(T // G):
                v.wait_ge(o_mm, g + 1)
                wait(v, fin_out[g % 2], 16 * (g // 2))
                nc.vector.tensor_tensor(fin[g % 2],
                                        sc[1][:, (g % 2) * CH:(g % 2 + 1) * CH].rearrange("p (t d) -> p t d", t=G),
                                        x[:, g * G:(g + 1) * G, :], ALU.add).then_inc(fin_ok, 1)


def rope_tables():
    inv_freq = (np.float32(1.0) / np.power(np.float32(10000.0), np.arange(0, DK, 2, dtype=np.float32)
                                           / np.float32(DK))).astype(np.float32)
    angle = np.arange(S, dtype=np.float32)[None, :] * np.tile(np.repeat(inv_freq, 2), H)[:, None]
    return np.cos(angle).astype(np.float32), np.sin(angle).astype(np.float32)


def constants():
    c = np.zeros((P, 4 * P), np.float32)
    i = np.arange(P)
    c[:, 0:P] = np.eye(P)
    c[:, P:2 * P] = i[:, None] < i[None, :]
    c[:, 2 * P:2 * P + H] = (i[:, None] // DK) == np.arange(H)[None, :]
    c[:, 3 * P:3 * P + E] = np.arange(E)
    c[:, 3 * P + E:3 * P + E + SLOT_TILES + 2] = np.arange(SLOT_TILES + 2)
    return c


INPUTS = ["L0_attn_x", "L0_attn_W_q", "L0_attn_W_k", "L0_attn_W_v", "L0_attn_W_o", "L0_ffn_Wg", "L0_ffn_gamma",
          "L0_ffn_beta", "L0_ffn_W1", "L0_ffn_b1", "L0_ffn_W2", "L0_ffn_b2"]


def kernel(**inputs):
    import concourse.bacc as bacc
    from concourse.bass_utils import run_bass_kernel_spmd

    nc = bacc.Bacc("TRN2", target_bir_lowering=False, num_devices=1)
    arrays, args = {}, []
    cos, sin = rope_tables()
    given = [(n, np.ascontiguousarray(inputs[n])) for n in INPUTS]
    given += [("rope_cos", cos), ("rope_sin", sin), ("shape_constants", constants())]
    for name, a in given:
        arrays[name] = a
        args.append(nc.dram_tensor(name, a.shape, mybir.dt.from_np(a.dtype), kind="ExternalInput").ap())
    args.append(nc.dram_tensor("out", (B, S, D), F32, kind="ExternalOutput").ap())
    build(nc, *args)
    return run_bass_kernel_spmd(nc, [arrays], core_ids=[0]).results[0]["out"]
```
